# Optimizing a Trainium2 kernel written in Bass

```python
import numpy as np
import jax
import jax.numpy as jnp

def _softmax(x, axis=-1):
    return jax.nn.softmax(x, axis=axis)

def _gelu(x):
    return jax.nn.gelu(x, approximate=True)

def _silu(x):
    return jax.nn.silu(x)

def _sigmoid(x):
    return jax.nn.sigmoid(x)

def _layernorm(x, axis=-1, eps=1e-05):
    m = jnp.mean(x, axis=axis, keepdims=True)
    v = jnp.var(x, axis=axis, keepdims=True)
    return (x - m) / jnp.sqrt(v + eps)

def _scatter_add(tgt, idx, src, axis=0):
    return tgt.at[idx].add(src)

def _segment_sum(src, seg, n):
    return jax.ops.segment_sum(src, seg, n)
kernel_name = 'mk_adj_resnorm_d1_adj_r2_81babd'

def setup_inputs(seed: int=0):
    np.random.seed(seed)
    _w = jnp.asarray

    def _rec_inputs():
        import jax
        import jax.numpy as jnp
        _gk = jax.random.key(seed)
        x = -0.000929 + 1 * jax.random.normal(jax.random.fold_in(_gk, 1), (2048, 256), jnp.float32)
        _w = (1.0 + jnp.arange(2048, dtype=jnp.float32)) ** (-0.5)
        _w = _w / _w.mean()
        _pij = jnp.clip(0.0078125 * _w[:, None] * _w[None, :], 0.0, 1.0)
        _a = jax.random.uniform(jax.random.fold_in(_gk, 2), (2048, 2048)) < _pij
        _af = _a.astype(jnp.float32)
        _af = _af * jax.random.uniform(jax.random.fold_in(_gk, 3), (2048, 2048), jnp.float32, 0.05, 5.22011)
        adj = _af
        return (x, adj)
    x, adj = _rec_inputs()

    def _L0_gnn_setup():
        import jax, jax.numpy as jnp
        import numpy as np
        N = 1024
        HID = 256
        H = 8
        key = jax.random.key(seed)
        ks = jax.random.split(key, 8)
        x = jax.random.normal(ks[0], (N, HID), dtype=jnp.float32)
        sp = jax.random.normal(ks[1], (N, N), dtype=jnp.float32)
        zero_mask = jax.random.uniform(ks[2], (N, N)) < 0.2
        spatial_encoding = jnp.where(zero_mask, 0.0, sp)
        edge_encoding = jax.random.normal(ks[3], (N, N), dtype=jnp.float32)
        s = 1.0 / np.sqrt(HID)
        Wq = jax.random.normal(ks[4], (HID, HID * H), dtype=jnp.float32) * s
        Wk = jax.random.normal(ks[5], (HID, HID * H), dtype=jnp.float32) * s
        Wv = jax.random.normal(ks[6], (HID, HID * H), dtype=jnp.float32) * s
        Wout = jax.random.normal(ks[7], (HID * H, HID), dtype=jnp.float32) * (1.0 / np.sqrt(HID * H))
        return {'x': x, 'spatial_encoding': spatial_encoding, 'edge_encoding': edge_encoding, 'Wq': Wq, 'Wk': Wk, 'Wv': Wv, 'Wout': Wout}
    _L0_gnn_all = _L0_gnn_setup()
    _L0_gnn_in = {k: v for k, v in _L0_gnn_all.items() if k in ('Wq', 'Wk', 'Wv', 'Wout')}
    del _L0_gnn_all
    return {'x': x, 'adj': adj, 'L0_gnn_Wq': _L0_gnn_in['Wq'], 'L0_gnn_Wk': _L0_gnn_in['Wk'], 'L0_gnn_Wv': _L0_gnn_in['Wv'], 'L0_gnn_Wout': _L0_gnn_in['Wout']}

def reference(x, adj, L0_gnn_Wq, L0_gnn_Wk, L0_gnn_Wv, L0_gnn_Wout):
    import jax
    import jax.numpy as jnp

    def _L0_gnn_ref(x, spatial_encoding, edge_encoding, Wq, Wk, Wv, Wout):
        import jax, jax.numpy as jnp
        import numpy as np
        N = 1024
        HID = 256
        H = 8
        n, d = x.shape
        h = Wq.shape[1] // d
        scale = d ** (-0.5)
        q = (x @ Wq).reshape(h, n, d)
        k = (x @ Wk).reshape(h, n, d)
        v = (x @ Wv).reshape(h, n, d)
        a = jnp.einsum('hnd,hmd->hnm', q, k) * scale
        a = a + spatial_encoding + edge_encoding
        mask = spatial_encoding == 0.0
        a = jnp.where(mask, -1000000.0, a)
        a = jax.nn.softmax(a, axis=-1)
        a = jnp.where(mask, 0.0, a)
        out = jnp.einsum('hnm,hmd->hnd', a, v)
        out = out.transpose(1, 0, 2).reshape(n, h * d)
        return out @ Wout
    x = _layernorm(x + _L0_gnn_ref(x, adj, adj, L0_gnn_Wq, L0_gnn_Wk, L0_gnn_Wv, L0_gnn_Wout), axis=-1)
    return x

_drawn_inputs = setup_inputs


def setup_inputs(seed=0):
    import zlib

    import numpy as np

    out = dict(_drawn_inputs(seed))
    spreads = {}
    factors = {}
    for name, (base, spread) in spreads.items():
        noise = np.random.default_rng([zlib.crc32(name.encode()), seed]).standard_normal(out[name].shape)
        drawn = base * np.exp(spread * noise) if base else spread * noise
        out[name] = jnp.asarray(drawn.astype(out[name].dtype))
    for name, factor in factors.items():
        out[name] = (out[name] * factor).astype(out[name].dtype)
    return out
```

```python
from contextlib import ExitStack

import concourse.bass as bass
from concourse import mybir

F32 = mybir.dt.float32
F32R = mybir.dt.float32r
ALU = mybir.AluOpType
ACT = mybir.ActivationFunctionType
AX = mybir.AxisListType

P = 128
BANK = 512
MASKED = -1000000.0
EPS = 1e-5
LOWEST = -3.0e38


def attention_layer_norm(nc, x, adj, wq, wk, wv, wout, out):
    n, d = x.shape
    H = wq.shape[1] // d
    R = n // H
    KT = d // P
    ST = R // P
    JT = n // P
    G = n // BANK
    JG = BANK // P
    QSCALE = 0.5 * float(d) ** -0.5
    assert KT == 2 and ST == 2 and R * KT == BANK and KT * d == BANK and G >= 2 and H >= 4 and H % 2 == 0

    adj_chunks = adj.rearrange("(s r b) (g j) -> b s g r j", s=ST, r=P, b=H, g=G)
    x_halves = x.rearrange("(s r b) e -> s r (b e)", s=ST, r=P, b=H)
    out_halves = out.rearrange("(s r b) e -> s r (b e)", s=ST, r=P, b=H)
    x_heads = x.rearrange("(h s p) e -> h p s e", h=H, s=ST)
    wk_blocks, wv_blocks = (w.rearrange("(t p) (c e) -> p t c e", t=KT, c=H) for w in (wk, wv))
    wq_blocks = wq.rearrange("(t p) (c e) -> c p t e", t=KT, c=H)
    wout_heads = wout.rearrange("(h t p) e -> h p t e", h=H, t=KT)

    ctx = ExitStack()
    with ctx:
        def sb(name, shape, dt=F32):
            return ctx.enter_context(nc.sbuf_tensor(name, shape, dt))

        def sem(name):
            return ctx.enter_context(nc.semaphore(name))

        bias_dram = nc.dram_tensor("bias_scratch", [H, ST, P, n], F32, kind="Internal").ap()

        ident = sb("ident", [P, P])
        wq_raw = sb("wq_raw", [P, KT, d])
        wk_raw = sb("wk_raw", [P, KT, H, d])
        wv_raw = sb("wv_raw", [P, KT, H, d])
        wo_raw = sb("wo_raw", [P, KT, d])
        xrows = sb("xrows", [P, ST, d])
        x_hi, x_lo = sb("x_hi", [P, KT, R], F32R), sb("x_lo", [P, KT, R], F32R)
        wo_hi, wo_lo = sb("wo_hi", [P, KT, d], F32R), sb("wo_lo", [P, KT, d], F32R)
        wq_hi, wq_lo = sb("wq_hi", [P, KT, d], F32R), sb("wq_lo", [P, KT, d], F32R)
        w_hi = [[sb(f"w_hi{m}{u}", [P, KT, d], F32R) for u in range(2)] for m in range(2)]
        w_lo = [[sb(f"w_lo{m}{u}", [P, KT, d], F32R) for u in range(2)] for m in range(2)]
        vt_hi = [sb(f"vt_hi{u}", [P, KT, R], F32R) for u in range(2)]
        vt_lo = [sb(f"vt_lo{u}", [P, KT, R], F32R) for u in range(2)]
        q_hi, q_lo = sb("q_hi", [P, KT, R], F32R), sb("q_lo", [P, KT, R], F32R)
        k_hi, k_lo = sb("k_hi", [P, KT, n], F32R), sb("k_lo", [P, KT, n], F32R)
        v_hl = sb("v_hl", [P, JT, 2, d], F32R)
        adj_raw = [sb(f"adj_raw{u}", [P, BANK]) for u in range(2)]
        masked = [sb(f"masked{u}", [P, H, BANK // H]) for u in range(2)]
        half_mask = sb("half_mask", [P, 1])
        bias = [sb(f"bias{u}", [P, n]) for u in range(2)]
        prob = [sb(f"prob{u}", [P, n]) for u in range(2)]
        pt_hi = [sb(f"pt_hi{u}", [P, BANK], F32R) for u in range(2)]
        pt_lo = [sb(f"pt_lo{u}", [P, BANK], F32R) for u in range(2)]
        acc = sb("acc", [P, ST, H, d])
        rowmax = [sb(f"rowmax{u}", [P, G]) for u in range(2)]
        negmax = [sb(f"negmax{u}", [P, 1]) for u in range(2)]
        expsum = [sb(f"expsum{u}", [P, G]) for u in range(2)]
        denom, rdenom, weight = sb("denom", [P, 1]), sb("rdenom", [P, 1]), sb("weight", [P, 1])
        mask_sum = sb("mask_sum", [P, G])
        mask_max = sb("mask_max", [P, 1])
        keep = sb("keep", [P, ST, H])
        stats = sb("stats", [P, ST, H, 6])
        moments = sb("moments", [P, ST, H, 2])
        veps, std, rstd = (sb(name, [P, ST, H]) for name in ("veps", "std", "rstd"))

        def bank(name):
            return ctx.enter_context(nc.psum_tensor(name, [P, BANK], F32))

        ps_s = [bank(f"ps_s{c}") for c in range(4)]
        ps_t = [bank(f"ps_t{u}") for u in range(2)]
        ps_o = [bank(f"ps_o{u}") for u in range(2)]

        ident_zero, ident_ready, half_mask_ready = sem("ident_zero"), sem("ident_ready"), sem("half_mask_ready")
        weights_in = [sem(f"weights_in{i}") for i in range(4)]
        acc_in, wq_in, xrows_in, wo_in = sem("acc_in"), sem("wq_in"), sem("xrows_in"), sem("wo_in")
        adj_in = [sem(f"adj_in{u}") for u in range(2)]
        masked_ready, bias_added = sem("masked_ready"), sem("bias_added")
        keep_steps = sem("keep_steps")
        bias_stored = [sem(f"bias_stored{u}") for u in range(2)]
        bias_in = [sem(f"bias_in{u}") for u in range(2)]
        xt_ps, xw_hi, xw_lo = sem("xt_ps"), sem("xw_hi"), sem("xw_lo")
        w_hi_ready, w_lo_ready = sem("w_hi_ready"), sem("w_lo_ready")
        kv_ps, kv_hi, kv_lo = sem("kv_ps"), sem("kv_hi"), sem("kv_lo")
        vp_ps, vp_hi, vp_lo = sem("vp_ps"), sem("vp_hi"), sem("vp_lo")
        wq_hi_ready, wq_lo_ready = sem("wq_hi_ready"), sem("wq_lo_ready")
        q_ps, q_hi_ready, q_lo_ready = sem("q_ps"), sem("q_hi_ready"), sem("q_lo_ready")
        scores_ps, logits_ready = sem("scores_ps"), sem("logits_ready")
        negmax_ready = [sem(f"negmax_ready{u}") for u in range(2)]
        exp_ready = sem("exp_ready")
        pt_ps, pt_hi_ready, pt_lo_ready = sem("pt_ps"), sem("pt_hi_ready"), sem("pt_lo_ready")
        pv_done = sem("pv_done")
        denom_steps = sem("denom_steps")
        out_added = [sem(f"out_added{u}") for u in range(2)]
        stats_ready, moments_ready = sem("stats_ready"), sem("moments_ready")
        veps_ready, std_ready, rstd_ready, normed = sem("veps_ready"), sem("std_ready"), sem("rstd_ready"), sem("normed")
        stored = sem("stored")
        pe_met, dve_met, pool_met = sem("pe_met"), sem("dve_met"), sem("pool_met")
        START = 1
        STARTED = {"pe": (xt_ps, q_ps), "pool": (wq_lo_ready, bias_added),
                   "dve": (keep_steps, xw_lo, vp_lo, logits_ready, *negmax_ready, *out_added)}

        block = ctx.enter_context(nc.Block())

        def group(h, b, r, g):
            return h * (2 * H * G) + b * (2 * G) + (r * G + g)

        def blk(h, c, u=0):
            return h * H + c + u

        def proj(h, pair, m, u):
            return h * (2 * H) + pair * 4 + (2 * m + u)

        PAIRS = H // 2
        LAST = PAIRS - 1
        KV = [(m, u) for m in range(2) for u in range(2)]
        ORDER = [("T", 0), ("T", 1), ("S", 0)]
        for c in range(1, G):
            ORDER += [("S", c)]
            ORDER += [("PV", c - 1), ("T", c + 1)] * (c < G - 1)
        ORDER += [("Q", 0), ("PV", G - 2), ("PV", G - 1)]
        MASKS = [("S", 0)] + [("T", g) for g in range(2, G)] + [("S", G - 1)]
        SCORES, NEXT_KV, NOTHING, QUERIES, NEXT_X = "scores", "next kv", "nothing", "queries", "next x"

        def key_block(t, c):
            return t[:, :, c, :] if len(t.shape) == 4 else t[:, :, bass.ds(c * R, R)]

        def halves(ps):
            return ps[:, :].rearrange("p (t s) -> p t s", t=2)

        def steps(engine, h, first, last, step):
            with engine.Fori(0, H - 1) as b:
                step(h, b, 0, SCORES, QUERIES, first, last)
                step(h, b, 1, SCORES, NOTHING, first, last)
            step(h, H - 1, 0, SCORES, NOTHING if last else NEXT_X, False, last)
            step(h, H - 1, 1, NOTHING if last else NEXT_KV, NOTHING, False, last)

        def heads(engine, head):
            head(0, True, False)
            with engine.Fori(1, H - 1) as h:
                head(h, False, False)
            head(H - 1, False, True)

        @block.sync
        def _(sp):
            def load_x(h):
                sp.wait_ge(xt_ps, h + START)
                sp.dma_start(xrows[:, :, :], x_heads[h]).then_inc(xrows_in, 16)
                sp.wait_ge(xw_lo, h * 2 + START)
                sp.dma_start(wo_raw[:, :, :], wout_heads[h]).then_inc(wo_in, 16)

            def load_wq(h, b):
                sp.wait_ge(wq_lo_ready, blk(h, b) + START)
                sp.dma_start(wq_raw[:, :, :], wq_blocks[b]).then_inc(wq_in, 16)

            def store_bias(b, r):
                sp.dma_start(bias_dram[b, r], bias[r][:, :]).then_inc(bias_stored[r], 16)

            def load_adj(b, r, chunks):
                for g in chunks:
                    sp.wait_ge(bias_added, group(0, b, r, g) - 1 + START)
                    sp.dma_start(adj_raw[g % 2][:, :], adj_chunks[b, r, g]).then_inc(adj_in[g % 2], 16)

            sp.dma_start(xrows[:, :, :], x_heads[0]).then_inc(xrows_in, 16)
            for i, (dst, src) in enumerate(((wk_raw, wk_blocks), (wv_raw, wv_blocks))):
                sp.dma_start(dst[:, :, 0:2, :], src[:, :, 0:2, :]).then_inc(weights_in[i], 16)
            sp.dma_start(wo_raw[:, :, :], wout_heads[0]).then_inc(wo_in, 16)
            sp.dma_start(wq_raw[:, :, :], wq_blocks[0]).then_inc(wq_in, 16)
            sp.dma_start(adj_raw[0][:, :], adj_chunks[0, 0, 0]).then_inc(adj_in[0], 16)
            sp.dma_start(adj_raw[1][:, :], adj_chunks[0, 0, 1]).then_inc(adj_in[1], 16)
            for i, (c0, c1) in enumerate(((2, 4), (4, H))):
                for dst, src in ((wk_raw, wk_blocks), (wv_raw, wv_blocks)):
                    if c1 > c0:
                        sp.dma_start(dst[:, :, c0:c1, :], src[:, :, c0:c1, :]).then_inc(weights_in[2 + i], 16)
            load_adj(0, 0, range(2, G))
            load_adj(0, 1, range(2))
            store_bias(0, 0)
            load_adj(0, 1, range(2, G))
            for s in range(ST):
                sp.dma_start(acc[:, s], x_halves[s].rearrange("r (b e) -> r b e", b=H)).then_inc(acc_in, 16)
            load_x(1)
            with sp.Fori(1, H) as b:
                load_wq(0, b)
                for r in range(2):
                    load_adj(b, r, range(2))
                    store_bias(b if r else b - 1, 1 - r)
                    load_adj(b, r, range(2, G))
            sp.wait_ge(bias_added, 2 * H * G + START)
            store_bias(H - 1, 1)
            for r in range(2):
                sp.wait_ge(bias_stored[r], 16 * H)

            def head(h, last):
                if not last:
                    load_x(h + 1)
                with sp.Fori(0, H) as b:
                    load_wq(h, b)
                    for r in range(2):
                        sp.wait_ge(negmax_ready[r], blk(h, b) + START)
                        sp.dma_start(bias[r][:, :], bias_dram[b, r]).then_inc(bias_in[r], 16)

            with sp.Fori(1, H - 1) as h:
                head(h, False)
            head(H - 1, True)
            for s in range(ST):
                sp.wait_ge(normed, H * (s + 1))
                sp.dma_start(out_halves[s], prob[s][:, :]).then_inc(stored, 16)
            sp.wait_ge(stored, 16 * ST)

        @block.gpsimd
        def _(pool):
            def cut_wq(h, b):
                pool.wait_ge(wq_in, blk(h, b, 1) * 16)
                pool.wait_ge(q_ps, blk(h, b) + START)
                pool.sem_inc(pool_met, 1)
                pool.tensor_copy(wq_hi[:, :, :], wq_raw[:, :, :]).then_inc(wq_hi_ready, 1)
                pool.wait_ge(wq_hi_ready, blk(h, b, 1))
                pool.tensor_tensor(wq_lo[:, :, :], wq_raw[:, :, :], wq_hi[:, :, :],
                                   ALU.subtract).then_inc(wq_lo_ready, 1)

            def add_bias(b, r, first=False):
                for g in range(G):
                    if g == 0 and not first:
                        pool.wait_ge(bias_stored[r], b * 16)
                        pool.wait_ge(negmax_ready[r], blk(0, b) + START)
                    pool.wait_ge(masked_ready, group(0, b, r, g) + 1)
                    w = BANK // H
                    pool.tensor_tensor(bias[r][:, :].rearrange("p (c k) -> p c k", c=H)[:, :, g * w:(g + 1) * w],
                                       adj_raw[g % 2][:, :].rearrange("p (k c) -> p c k", c=H),
                                       masked[g % 2][:, :, :], ALU.add).then_inc(bias_added, 1)

            for s in STARTED["pool"]:
                pool.sem_inc(s, START)
            pool.memset(half_mask[:, :], 0.5 * MASKED).then_inc(half_mask_ready, 1)
            pool.memset(ident[:, :], 0.0).then_inc(ident_zero, 1)
            pool.wait_ge(ident_zero, 1)
            pool.affine_select(out=ident[:, :], in_=ident[:, :], compare_op=ALU.not_equal, fill=1.0, base=0,
                               pattern=[[-1, P]], channel_multiplier=1).then_inc(ident_ready, 1)
            cut_wq(0, 0)
            for r in range(2):
                add_bias(0, r, first=True)
            with pool.Fori(1, H) as b:
                cut_wq(0, b)
                for r in range(2):
                    add_bias(b, r)
            with pool.Fori(1, H) as h:
                with pool.Fori(0, H) as b:
                    cut_wq(h, b)

        @block.tensor
        def _(pe):
            def product(ps, lhs, rhs, tiles):
                terms = [(a, b, t) for t in range(tiles) for a, b in ((0, 0), (0, 1), (1, 0))]
                for i, (a, b, t) in enumerate(terms):
                    last = pe.matmul(ps, lhs(a, t), rhs(b, t), start=(i == 0), stop=(i == len(terms) - 1))
                return last

            def x_part(b, t):
                return (x_hi, x_lo)[b][:, t, :]

            def transpose_x(h):
                pe.wait_ge(xrows_in, (h + 1) * 16)
                for t in range(KT):
                    for s in range(ST):
                        last = pe.transpose(ps_s[0][:, t * R + s * P:t * R + (s + 1) * P],
                                            xrows[:, s, t * P:(t + 1) * P], ident[:, :])
                last.then_inc(xt_ps, 1)

            def project_kv(h, pair, m, u):
                pe.wait_ge(w_lo_ready, proj(h, pair, m, u) + 1)
                for t in range(KT):
                    last = product(ps_s[2 * m + u][:, t * R:(t + 1) * R],
                                   lambda a, k: (w_hi, w_lo)[a][m][u][:, k, t * P:(t + 1) * P], x_part, KT)
                last.then_inc(kv_ps, 1)

            def project_vout(h, pair, u):
                pe.wait_ge(kv_lo, proj(h, pair, 1, u) + 1)
                if u == 0:
                    pe.wait_ge(vp_lo, blk(h, pair * 2) + START)
                for s in range(ST):
                    last = product(ps_o[u][:, s * d:(s + 1) * d],
                                   lambda a, k: (vt_hi, vt_lo)[a][u][:, k, s * P:(s + 1) * P],
                                   lambda b, k: (wo_hi, wo_lo)[b][:, k, :], KT)
                last.then_inc(vp_ps, 1)

            def project_q(h, b, ps):
                pe.wait_ge(wq_lo_ready, blk(h, b, 1) + START)
                for t in range(KT):
                    last = product(ps[:, t * R:(t + 1) * R],
                                   lambda a, k: (wq_hi, wq_lo)[a][:, k, t * P:(t + 1) * P], x_part, KT)
                last.then_inc(q_ps, 1)

            def scores(r, c):
                product(ps_s[c][:, :], lambda a, k: (q_hi, q_lo)[a][:, k, r * P:(r + 1) * P],
                        lambda b, k: (k_hi, k_lo)[b][:, k, c * BANK:(c + 1) * BANK], KT).then_inc(scores_ps, 1)

            def transposes(h, b, r, g):
                pe.wait_ge(exp_ready, group(h, b, r, g) + 1)
                for j in range(JG):
                    k = (g * JG + j) * P
                    last = pe.transpose(ps_t[g % 2][:, j * P:(j + 1) * P], prob[r][:, k:k + P], ident[:, :])
                last.then_inc(pt_ps, 1)

            def weigh_values(h, b, r, g):
                if g == 0:
                    pe.wait_ge(out_added[r], blk(h, b) + START)
                    pe.wait_ge(vp_lo, blk(h, H) + START)
                pe.wait_ge(pt_lo_ready, group(h, b, r, g) + 1)
                for j in range(JG):
                    k = g * JG + j
                    hi, lo = (t[g % 2][:, j * P:(j + 1) * P] for t in (pt_hi, pt_lo))
                    both = (ps_o[r][:, :], hi, v_hl[:, k, :, :].rearrange("p a e -> p (a e)"))
                    cross = (ps_o[r][:, d:2 * d], lo, v_hl[:, k, 0, :])
                    if k == 0:
                        pe.matmul(*both, start=True, stop=False)
                        last = pe.matmul(*cross, start=False, stop=False)
                    else:
                        pe.matmul(*cross, start=False, stop=False)
                        last = pe.matmul(*both, start=False, stop=(k == JT - 1))
                last.then_inc(pv_done, 1)

            def step(h, b, r, in_s, in_q, first, last):
                for what, g in ORDER:
                    if what == "T":
                        transposes(h, b, r, g)
                    elif what == "PV":
                        weigh_values(h, b, r, g)
                    elif what == "S" and in_s == SCORES:
                        if r == 1 and g == 0:
                            pe.wait_ge(q_lo_ready, blk(h, b, 2))
                        pe.wait_ge(logits_ready, group(h, b, r, g) + 1 + START)
                        scores(1 - r, g)
                    elif what == "S" and in_s == NEXT_KV:
                        for m, u in KV[g * 4 // G:(g + 1) * 4 // G]:
                            if m == u == 0:
                                pe.wait_ge(xw_lo, h * 2 + 3 + START)
                                pe.wait_ge(logits_ready, group(h, H, 0, 0) + START)
                            project_kv(h + 1, 0, m, u)
                    elif what == "Q" and in_q != NOTHING:
                        pe.wait_ge(logits_ready, group(h, b, r + 1, 0) + 1 + START)
                        if in_q == QUERIES:
                            project_q(h, b + 1, ps_s[0])
                        else:
                            transpose_x(h + 1)

            def head(h, first, last):
                for u in range(2):
                    pe.wait_ge(out_added[u], blk(h, 0) + START)
                    if u == 0:
                        pe.wait_ge(xw_lo, h * 2 + 2 + START)
                    project_vout(h, 0, u)
                if LAST > 1:
                    with pe.Fori(1, LAST) as pair:
                        for m, u in KV:
                            project_kv(h, pair, m, u)
                        for u in range(2):
                            project_vout(h, pair, u)
                for m, u in KV:
                    if (m, u) == (1, 0):
                        pe.wait_ge(vp_lo, blk(h, 2 * LAST) + START)
                        project_q(h, 0, ps_o[0])
                    project_kv(h, LAST, m, u)
                pe.wait_ge(q_lo_ready, blk(h, 0, 1))
                for c in range(G):
                    if c != 1:
                        pe.wait_ge(kv_lo, proj(h, LAST, 0, max(c, 1)) + 1)
                    scores(0, c)
                for u in range(2):
                    project_vout(h, LAST, u)
                steps(pe, h, first, last, step)

            for s in STARTED["pe"]:
                pe.sem_inc(s, START)
            pe.wait_ge(ident_ready, 1)
            transpose_x(0)
            pe.wait_ge(xw_lo, 1 + START)
            for m, u in KV:
                project_kv(0, 0, m, u)
            heads(pe, head)

        @block.scalar
        def _(act):
            def cut_weight(m, u, source_pair):
                act.activation(w_hi[m][u][:, :, :], key_block((wk_raw, wv_raw)[m], source_pair * 2 + u),
                               ACT.Copy).then_inc(w_hi_ready, 1)

            def cut_x(h):
                act.wait_ge(xt_ps, h + 1 + START)
                act.activation(x_hi[:, :, :], halves(ps_s[0]), ACT.Copy).then_inc(xw_hi, 1)

            def cut_wout(h):
                act.wait_ge(wo_in, (h + 1) * 16)
                act.activation(wo_hi[:, :, :], wo_raw[:, :, :], ACT.Copy).then_inc(xw_hi, 1)

            def cut_kv(h, pair, m, u, next_pair):
                act.wait_ge(kv_ps, proj(h, pair, m, u) + 1)
                dst = vt_hi[u][:, :, :] if m else key_block(k_hi, pair * 2 + u)
                act.activation(dst, halves(ps_s[2 * m + u]), ACT.Copy).then_inc(kv_hi, 1)
                if next_pair is not None:
                    cut_weight(m, u, next_pair)

            def cut_vout(h, pair, u):
                act.wait_ge(vp_ps, blk(h, pair * 2, u + 1))
                act.activation(v_hl[:, bass.ds((pair * 2 + u) * ST, ST), 0, :], halves(ps_o[u]), ACT.Copy).then_inc(vp_hi, 1)

            def cut_q(h, b, ps):
                act.wait_ge(q_ps, blk(h, b, 1) + START)
                act.activation(q_hi[:, :, :], halves(ps), ACT.Copy, scale=QSCALE).then_inc(q_hi_ready, 1)

            def exps(h, b, r, c):
                if c == 0:
                    act.wait_ge(negmax_ready[r], blk(h, b, 1) + START)
                chunk = prob[r][:, c * BANK:(c + 1) * BANK]
                act.activation(chunk, chunk, ACT.Exp, bias=negmax[r][:, :], scale=2.0,
                               accum_out=expsum[r][:, c:c + 1]).then_inc(exp_ready, 1)

            def step(h, b, r, in_s, in_q, first, last):
                for what, g in ORDER:
                    if what == "T":
                        act.wait_ge(pt_ps, group(h, b, r, g) + 1)
                        act.activation(pt_hi[g % 2][:, :], ps_t[g % 2][:, :], ACT.Copy).then_inc(pt_hi_ready, 1)
                    elif what == "S" and in_s == NEXT_KV:
                        for m, u in KV[g * 4 // G:(g + 1) * 4 // G]:
                            cut_kv(h + 1, 0, m, u, 1)
                for c in range(G):
                    if in_s == SCORES:
                        exps(h, b if r == 0 else b + 1, 1 - r, c)
                    if in_q == QUERIES and c == 1:
                        cut_q(h, b + 1, ps_s[0])
                    if in_q == NEXT_X and c == 1:
                        cut_x(h + 1)
                        cut_wout(h + 1)

            def head(h, first, last):
                for u in range(2):
                    cut_vout(h, 0, u)
                if LAST > 1:
                    with act.Fori(1, LAST) as pair:
                        for m, u in KV:
                            cut_kv(h, pair, m, u, pair + 1)
                        for u in range(2):
                            cut_vout(h, pair, u)
                for m, u in KV:
                    if (m, u) == (1, 0):
                        cut_q(h, 0, ps_o[0])
                    cut_kv(h, LAST, m, u, None if last else 0)
                for c in range(G):
                    exps(h, 0, 0, c)
                    if c < 2:
                        cut_vout(h, LAST, c)
                steps(act, h, first, last, step)

            cut_x(0)
            for m, u in KV:
                act.wait_ge(weights_in[m], 16)
                cut_weight(m, u, 0)
            cut_wout(0)
            act.wait_ge(weights_in[2], 16 * 2)
            for m, u in KV:
                cut_kv(0, 0, m, u, 1)
            if H > 4:
                act.wait_ge(weights_in[3], 16 * 2)
            heads(act, head)
            act.wait_ge(veps_ready, 1)
            act.activation(std[:, :, :], veps[:, :, :], ACT.Sqrt).then_inc(std_ready, 1)

        @block.vector
        def _(dve):
            def cut_weight(index, m, u, source_pair):
                dve.wait_ge(w_hi_ready, index + 1)
                dve.tensor_tensor(w_lo[m][u][:, :, :], key_block((wk_raw, wv_raw)[m], source_pair * 2 + u),
                                  w_hi[m][u][:, :, :], ALU.subtract).then_inc(w_lo_ready, 1)

            def cut_x(h):
                dve.wait_ge(xw_hi, h * 2 + 1)
                dve.tensor_tensor(x_lo[:, :, :], halves(ps_s[0]), x_hi[:, :, :], ALU.subtract).then_inc(xw_lo, 1)

            def cut_wout(h):
                dve.wait_ge(xw_hi, h * 2 + 2)
                dve.tensor_tensor(wo_lo[:, :, :], wo_raw[:, :, :], wo_hi[:, :, :], ALU.subtract).then_inc(xw_lo, 1)

            def cut_kv(h, pair, m, u, next_pair):
                dve.wait_ge(kv_hi, proj(h, pair, m, u) + 1)
                hi, dst = ((vt_hi[u][:, :, :], vt_lo[u][:, :, :]) if m else
                           (key_block(k_hi, pair * 2 + u), key_block(k_lo, pair * 2 + u)))
                dve.tensor_tensor(dst, halves(ps_s[2 * m + u]), hi, ALU.subtract).then_inc(kv_lo, 1)
                if next_pair is not None:
                    cut_weight(proj(h, pair, m, u) + 4, m, u, next_pair)

            def cut_vout(h, pair, u):
                dve.wait_ge(vp_hi, blk(h, pair * 2, u + 1))
                tiles = bass.ds((pair * 2 + u) * ST, ST)
                dve.tensor_tensor(v_hl[:, tiles, 1, :], halves(ps_o[u]), v_hl[:, tiles, 0, :],
                                  ALU.subtract).then_inc(vp_lo, 1)

            def cut_q(h, b, ps):
                dve.wait_ge(q_hi_ready, blk(h, b, 1))
                dve.scalar_tensor_tensor(q_lo[:, :, :], halves(ps), QSCALE, q_hi[:, :, :],
                                         ALU.mult, ALU.subtract).then_inc(q_lo_ready, 1)

            def mask(b, r, g):
                dve.wait_ge(adj_in[g % 2], (group(0, b, r, g - g % 2) + 2) * 8)
                if not (isinstance(b, int) and b == r == 0 and g < 2):
                    dve.wait_ge(bias_added, group(0, b, r, g) - 1 + START)
                if g == 0:
                    dve.wait_ge(keep_steps, b * 4 + 2 * r + START)
                dve.scalar_tensor_tensor(masked[g % 2][:, :, :], adj_raw[g % 2][:, :].rearrange("p (k c) -> p c k", c=H), 0.0,
                                         half_mask[:, 0:1].to_broadcast([P, BANK]).rearrange("p (c k) -> p c k", c=H),
                                         ALU.is_equal, ALU.mult,
                                         accum_out=mask_sum[:, g:g + 1]).then_inc(masked_ready, 1)
                if g == G - 1:
                    dve.wait_ge(masked_ready, group(0, b, r, G))
                    dve.tensor_reduce(mask_max[:, :], mask_sum[:, :], AX.X, ALU.max).then_inc(keep_steps, 1)
                    dve.wait_ge(keep_steps, b * 4 + (2 * r + 1) + START)
                    dve.tensor_scalar(keep[:, r, bass.ds(b, 1)], mask_max[:, :], 0.5 * MASKED * BANK, None,
                                      ALU.is_gt).then_inc(keep_steps, 1)

            def logits(h, b, r, c, first):
                if c == 0 and first:
                    dve.wait_ge(bias_added, group(0, b, r, G) + START)
                elif c == 0:
                    dve.wait_ge(bias_in[r], blk(h - 1, b, 1) * 16)
                if c:
                    dve.wait_ge(logits_ready, group(h, b, r, c) + START)
                dve.wait_ge(scores_ps, group(h, b, r, c) + 1)
                dve.sem_inc(dve_met, 1)
                cols = slice(c * BANK, (c + 1) * BANK)
                dve.tensor_tensor_reduce(prob[r][:, cols], ps_s[c][:, :], bias[r][:, cols], 1.0,
                                         rowmax[r][:, c - 1:c] if c else LOWEST, ALU.add, ALU.max,
                                         rowmax[r][:, c:c + 1]).then_inc(logits_ready, 1)

            def negate_max(h, b, r):
                dve.wait_ge(logits_ready, group(h, b, r, G) + START)
                dve.tensor_scalar(negmax[r][:, :], rowmax[r][:, G - 1:G], -2.0, None, ALU.mult).then_inc(negmax_ready[r], 1)

            def add_tile(h, b, r):
                before = h * (2 * H * 4) + b * 8 + r * 4
                dve.wait_ge(out_added[1 - r], blk(h, b, r) + START)
                dve.tensor_reduce(denom[:, :], expsum[r][:, :], AX.X, ALU.add).then_inc(denom_steps, 1)
                dve.wait_ge(denom_steps, before + 1)
                dve.reciprocal(rdenom[:, :], denom[:, :]).then_inc(denom_steps, 1)
                dve.wait_ge(denom_steps, before + 2)
                dve.tensor_tensor(weight[:, :], rdenom[:, :], keep[:, r, bass.ds(b, 1)], ALU.mult).then_inc(denom_steps, 1)
                dve.wait_ge(denom_steps, before + 3)
                dve.wait_ge(pv_done, group(h, b, r, G))
                a = acc[:, r, b, :]
                dve.scalar_tensor_tensor(a, ps_o[r][:, d:2 * d], weight[:, :], a,
                                         ALU.mult, ALU.add).then_inc(denom_steps, 1)
                dve.wait_ge(denom_steps, before + 4)
                dve.scalar_tensor_tensor(a, ps_o[r][:, 0:d], weight[:, :], a,
                                         ALU.mult, ALU.add).then_inc(out_added[r], 1)

            def row_stats(b, r):
                dve.wait_ge(out_added[r], blk(H - 1, b, 1) + START)
                dve.bn_stats(stats[:, r, b, :], acc[:, r, b, :]).then_inc(stats_ready, 1)

            def step(h, b, r, in_s, in_q, first, last):
                nb = b if r == 0 else b + 1
                in_first_head = isinstance(h, int) and h == 0
                for what, g in ORDER:
                    if what == "T":
                        dve.wait_ge(pt_hi_ready, group(h, b, r, g) + 1)
                        dve.tensor_tensor(pt_lo[g % 2][:, :], ps_t[g % 2][:, :], pt_hi[g % 2][:, :],
                                          ALU.subtract).then_inc(pt_lo_ready, 1)
                    elif what == "S" and in_s == SCORES:
                        logits(h, nb, 1 - r, g, in_first_head)
                        if g == G - 1:
                            negate_max(h, nb, 1 - r)
                    elif what == "S" and in_s == NEXT_KV:
                        for m, u in KV[g * 4 // G:(g + 1) * 4 // G]:
                            cut_kv(h + 1, 0, m, u, 1)
                    elif what == "Q" and in_q == QUERIES:
                        cut_q(h, b + 1, ps_s[0])
                    elif what == "Q" and in_q == NEXT_X:
                        cut_x(h + 1)
                        cut_wout(h + 1)
                    if first and (what, g) in MASKS:
                        mask(b + 1, r, MASKS.index((what, g)))
                add_tile(h, b, r)
                if last:
                    row_stats(b, r)

            def head(h, first, last):
                for u in range(2):
                    cut_vout(h, 0, u)
                def pair_of_blocks(pair):
                    for m, u in KV:
                        cut_kv(h, pair, m, u, pair + 1)
                    for u in range(2):
                        cut_vout(h, pair, u)

                chunks = [(r, g) for r in range(2) for g in range(G)] if first else []
                if first:
                    for pair in range(1, LAST):
                        for r, g in chunks[:2]:
                            mask(0, r, g)
                        del chunks[:2]
                        pair_of_blocks(pair)
                    while chunks and chunks[0][0] == 0:
                        mask(0, *chunks.pop(0))
                elif LAST > 1:
                    with dve.Fori(1, LAST) as pair:
                        pair_of_blocks(pair)
                for m, u in KV:
                    if (m, u) == (1, 0):
                        cut_q(h, 0, ps_o[0])
                    cut_kv(h, LAST, m, u, None if last else 0)
                for c in range(G):
                    logits(h, 0, 0, c, first)
                negate_max(h, 0, 0)
                for u in range(2):
                    cut_vout(h, LAST, u)
                for r, g in chunks:
                    mask(0, r, g)
                if first:
                    dve.wait_ge(acc_in, 16 * ST)
                steps(dve, h, first, last, step)

            for s in STARTED["dve"]:
                dve.sem_inc(s, START)
            dve.wait_ge(half_mask_ready, 1)
            cut_x(0)
            for m, u in KV:
                cut_weight(2 * m + u, m, u, 0)
            cut_wout(0)
            for m, u in KV:
                cut_kv(0, 0, m, u, 1)
            heads(dve, head)

            tiles = [(r, b) for r in range(ST) for b in range(H)]
            dve.wait_ge(stats_ready, JT)
            for r, b in tiles:
                dve.bn_aggr(moments[:, r, b, :], stats[:, r, b, :]).then_inc(moments_ready, 1)
            dve.wait_ge(moments_ready, JT)
            dve.tensor_scalar(veps[:, :, :], moments[:, :, :, 1], EPS, None, ALU.add).then_inc(veps_ready, 1)
            dve.wait_ge(std_ready, 1)
            dve.reciprocal(rstd[:, :, :], std[:, :, :]).then_inc(rstd_ready, 1)
            dve.wait_ge(rstd_ready, 1)
            for r, b in tiles:
                dve.tensor_scalar(prob[r][:, b * d:(b + 1) * d], acc[:, r, b, :], moments[:, r, b, 0:1],
                                  rstd[:, r, b:b + 1], ALU.subtract, ALU.mult).then_inc(normed, 1)


_INPUTS = ["x", "adj", "L0_gnn_Wq", "L0_gnn_Wk", "L0_gnn_Wv", "L0_gnn_Wout"]


def kernel(**inputs):
    import numpy as np
    import concourse.bacc as bacc
    from concourse.bass_utils import run_bass_kernel_spmd

    nc = bacc.Bacc("TRN2", target_bir_lowering=False, num_devices=1)
    arrays, args = {}, []
    for name in _INPUTS:
        a = np.ascontiguousarray(inputs[name])
        arrays[f"in_{name}"] = a
        args.append(nc.dram_tensor(f"in_{name}", a.shape, mybir.dt.from_np(a.dtype), kind="ExternalInput").ap())
    out = nc.dram_tensor("out", arrays["in_x"].shape, F32, kind="ExternalOutput").ap()
    attention_layer_norm(nc, *args, out)
    r = run_bass_kernel_spmd(nc, [arrays], core_ids=[0])
    return r.results[0]["out"]
```

```python
from contextlib import ExitStack

import concourse.bass as bass
from concourse import mybir

F32 = mybir.dt.float32
F32R = mybir.dt.float32r
ALU = mybir.AluOpType
ACT = mybir.ActivationFunctionType
AX = mybir.AxisListType

P = 128
BANK = 512
MASKED = -1000000.0
EPS = 1e-5


def attention_layer_norm(nc, x, adj, wq, wk, wv, wout, out):
    n, d = x.shape
    H = wq.shape[1] // d
    R = n // H
    KT = d // P
    ST = R // P
    JT = n // P
    CHUNK = P * H
    QUADS = H // 4
    RING = 4
    ONES = 2
    QSCALE = 0.5 * float(d) ** -0.5
    assert KT == 2 and ST == 2 and ST * R == BANK and KT * d == BANK and H % 4 == 0

    adj_chunks = adj.rearrange("(s r b) (g j) -> b s g r j", s=ST, r=P, b=H, g=ST)
    x_halves = x.rearrange("(s r b) e -> s r (b e)", s=ST, r=P, b=H)
    out_halves = out.rearrange("(s r b) e -> s r (b e)", s=ST, r=P, b=H)
    x_heads = x.rearrange("(h s p) e -> h p s e", h=H, s=ST)
    w_pairs = [w.rearrange("(t p) (c u e) -> c p t u e", t=KT, u=2, e=d) for w in (wk, wv)]
    wq_blocks = wq.rearrange("(t p) (c e) -> c p t e", t=KT, c=H)
    wout_heads = wout.rearrange("(h t p) e -> h p t e", h=H, t=KT)

    ctx = ExitStack()
    with ctx:
        def sb(name, shape, dt=F32):
            return ctx.enter_context(nc.sbuf_tensor(name, shape, dt))

        def sem(name):
            return ctx.enter_context(nc.semaphore(name))

        bias_dram = nc.dram_tensor("bias_scratch", [H, H, P, ST, ST, P], F32, kind="Internal").ap()

        ident = sb("ident", [P, P])
        wq_raw = sb("wq_raw", [P, KT, d])
        w_raw = [sb(f"w_raw{m}", [P, KT, 2, d]) for m in range(2)]
        wo_raw = sb("wo_raw", [P, KT, d])
        xrows = sb("xrows", [P, ST, d])
        x_hi, x_lo = sb("x_hi", [P, KT, R], F32R), sb("x_lo", [P, KT, R], F32R)
        wo_hi, wo_lo = sb("wo_hi", [P, KT, d], F32R), sb("wo_lo", [P, KT, d], F32R)
        wq_hi, wq_lo = sb("wq_hi", [P, KT, d], F32R), sb("wq_lo", [P, KT, d], F32R)
        w_hi = [[sb(f"w_hi{m}{u}", [P, KT, d], F32R) for u in range(2)] for m in range(2)]
        w_lo = [[sb(f"w_lo{m}{u}", [P, KT, d], F32R) for u in range(2)] for m in range(2)]
        vt_hi = [sb(f"vt_hi{u}", [P, KT, R], F32R) for u in range(2)]
        vt_lo = [sb(f"vt_lo{u}", [P, KT, R], F32R) for u in range(2)]
        q_hi, q_lo = sb("q_hi", [P, KT, R], F32R), sb("q_lo", [P, KT, R], F32R)
        k_hi, k_lo = sb("k_hi", [P, KT, n], F32R), sb("k_lo", [P, KT, n], F32R)
        v_hi = sb("v_hi", [P, JT, d + ONES], F32R)
        v_lo = sb("v_lo", [P, JT, d], F32R)
        adj_raw = [sb(f"adj_raw{u}", [P, CHUNK]) for u in range(2)]
        masked = [sb(f"masked{u}", [P, CHUNK]) for u in range(2)]
        half_mask, ones = sb("half_mask", [P, 1]), sb("ones", [P, 1])
        bias_t = [sb(f"bias_t{u}", [P, BANK]) for u in range(2)]
        bias = [sb(f"bias{u}", [P, 2, BANK]) for u in range(2)]
        logits_sb = sb("logits", [P, H, BANK])
        prob = sb("prob", [P, H, BANK])
        pt_hi = [sb(f"pt_hi{u}", [P, BANK], F32R) for u in range(2)]
        pt_lo = [sb(f"pt_lo{u}", [P, BANK], F32R) for u in range(2)]
        acc = sb("acc", [P, ST, H, d])
        keymax = sb("keymax", [P, BANK])
        rowmax = sb("rowmax", [P, ST])
        maxes = sb("maxes", [P, 2, R])
        rdenom, weight = sb("rdenom", [P, ST]), sb("weight", [P, ST])
        mask_sum = sb("mask_sum", [P, ST])
        mask_max = sb("mask_max", [P, 1])
        keep = sb("keep", [P, ST, H])
        stats = sb("stats", [P, ST, H, 6])
        moments = sb("moments", [P, ST, H, 2])
        veps, std, rstd = (sb(name, [P, ST, H]) for name in ("veps", "std", "rstd"))

        def bank(name):
            return ctx.enter_context(nc.psum_tensor(name, [P, BANK], F32))

        ps_s = [bank(f"ps_s{c}") for c in range(RING)]
        ps_o = [bank(f"ps_o{u}") for u in range(2)]
        ps_m = bank("ps_m")
        ps_b = bank("ps_b")

        ident_zero, ident_ready, half_mask_ready = sem("ident_zero"), sem("ident_ready"), sem("half_mask_ready")
        ones_ready = sem("ones_ready")
        w_in = [sem(f"w_in{m}") for m in range(2)]
        acc_in, wq_in, xrows_in, wo_in = sem("acc_in"), sem("wq_in"), sem("xrows_in"), sem("wo_in")
        adj_in = [sem(f"adj_in{u}") for u in range(2)]
        masked_ready, bias_added = sem("masked_ready"), sem("bias_added")
        bias_ps, bias_cut = sem("bias_ps"), sem("bias_cut")
        keep_steps = sem("keep_steps")
        bias_stored = [sem(f"bias_stored{u}") for u in range(2)]
        bias_in = [sem(f"bias_in{u}") for u in range(2)]
        xt_ps, xw_hi, xw_lo = sem("xt_ps"), sem("xw_hi"), sem("xw_lo")
        w_hi_ready, w_lo_ready = sem("w_hi_ready"), sem("w_lo_ready")
        kv_ps, kv_hi, kv_lo = sem("kv_ps"), sem("kv_hi"), sem("kv_lo")
        vp_ps, vp_hi, vp_lo = sem("vp_ps"), sem("vp_hi"), sem("vp_lo")
        wq_hi_ready, wq_lo_ready = sem("wq_hi_ready"), sem("wq_lo_ready")
        q_ps, q_hi_ready, q_lo_ready = sem("q_ps"), sem("q_hi_ready"), sem("q_lo_ready")
        scores_ps, logits_ready, keymax_ready = sem("scores_ps"), sem("logits_ready"), sem("keymax_ready")
        keymax_ps, rowmax_ready, maxes_ps, maxes_ready = (
            sem("keymax_ps"), sem("rowmax_ready"), sem("maxes_ps"), sem("maxes_ready"))
        shifted, exp_ready = sem("shifted"), sem("exp_ready")
        pt_hi_ready, pt_lo_ready = sem("pt_hi_ready"), sem("pt_lo_ready")
        pv_done = sem("pv_done")
        rdenom_ready, weight_ready = sem("rdenom_ready"), sem("weight_ready")
        out_added = sem("out_added")
        stats_ready, moments_ready = sem("stats_ready"), sem("moments_ready")
        veps_ready, std_ready, rstd_ready, normed = sem("veps_ready"), sem("std_ready"), sem("rstd_ready"), sem("normed")
        stored = sem("stored")
        sp_met, pool_met = sem("sp_met"), sem("pool_met")
        START = 2
        STARTED = {"pe": (xt_ps, q_ps, pv_done), "pool": (wq_lo_ready, bias_added),
                   "act": (maxes_ready, bias_cut),
                   "dve": (keep_steps, xw_lo, vp_lo, logits_ready, out_added)}

        block = ctx.enter_context(nc.Block())

        def unit(h, b, c):
            return h * (H * H) + b * H + c

        def blk(h, c, u=0):
            return h * H + c + u

        def proj(h, pair, m, u):
            return h * (2 * H) + pair * 4 + (2 * m + u)

        PAIRS = H // 2
        LAST = PAIRS - 1
        KV = [(m, u) for m in range(2) for u in range(2)]
        LAG = 4
        ORDER = [("S", 0), ("S", 1)]
        for c in range(2, H):
            ORDER += [("PV", c - 2)] * (c - 2 < H - LAG) + [("S", c)]
        ORDER += [("Q", 0), ("PV", H - 4), ("MT", 0), ("PV", H - 3), ("MB", 0), ("PV", H - 2), ("PV", H - 1)]
        CUT_AT = {("S", 1): 1} | {ORDER[ORDER.index(("PV", c - 2)) + 1]: c for c in range(2, H)}
        PLACES = [item for item in ORDER if item[0] not in ("MT", "MB")]
        BIAS_AT = ([("S", c) for c in range(H - 3, H)] + [("Q", 0)] + [("PV", c) for c in range(H - 4, H)])[-H:]
        MASK_AT = [("S", 1), ("S", H // 2 - 1)] + [PLACES[PLACES.index(BIAS_AT[k * QUADS - 1]) + 1] for k in (1, 2)]
        SCORES, NEXT_KV, NOTHING, QUERIES, NEXT_X = "scores", "next kv", "nothing", "queries", "next x"
        CHUNKS = [(s, g) for s in range(ST) for g in range(ST)]

        def halves(ps):
            return ps[:, 0:KT * R].rearrange("p (t s) -> p t s", t=2)

        def steps(engine, h, first, last, step):
            with engine.Fori(0, H - 3) as b:
                step(h, b, SCORES, QUERIES, True, first, last)
            step(h, H - 3, SCORES, QUERIES, not last, first, last)
            step(h, H - 2, SCORES, NOTHING if last else NEXT_X, False, False, last)
            step(h, H - 1, NOTHING if last else NEXT_KV, NOTHING, False, False, last)

        def heads(engine, head):
            head(0, True, False)
            with engine.Fori(1, H - 1) as h:
                head(h, False, False)
            head(H - 1, False, True)

        def phase_a(engine, h, first, v_out, kv, queries, scores, maxes, spare):
            def pair_of_blocks(pair):
                for u in range(2):
                    kv(h, pair, 0, u)
                    spare()
                for u in range(2):
                    v_out(h, pair - 1, u)
                    spare()
                for u in range(2):
                    kv(h, pair, 1, u)
                    spare()

            if first:
                for pair in range(1, LAST):
                    pair_of_blocks(pair)
            elif LAST > 1:
                pair_of_blocks(1)
                if LAST > 2:
                    with engine.Fori(2, LAST) as pair:
                        pair_of_blocks(pair)
            queries(h, 0)
            spare()
            for u in range(2):
                kv(h, LAST, 0, u)
                spare()
            for u in range(2):
                v_out(h, LAST - 1, u)
                spare()
            for c in range(H):
                scores(h, 0, c)
                spare()
            kv(h, LAST, 1, 0)
            kv(h, LAST, 1, 1)
            maxes("MT", h, 0)
            queries(h, 1)
            maxes("MB", h, 0)
            v_out(h, LAST, 0)
            v_out(h, LAST, 1)

        def v_bank(pair, m, u):
            return ps_s[u] if isinstance(pair, int) and pair == LAST else ps_s[2 * m + u]

        def spares(do):
            left = list(range(2 * H))
            return lambda: left and do(left.pop(0))

        def group_chunk(i):
            return i // QUADS, i % QUADS * 4

        @block.sync
        def _(sp):
            def load_x(h):
                sp.wait_ge(xt_ps, h + START)
                sp.dma_start(xrows[:, :, :], x_heads[h]).then_inc(xrows_in, 16)
                sp.wait_ge(xw_lo, h * 2 + START)
                sp.dma_start(wo_raw[:, :, :], wout_heads[h]).then_inc(wo_in, 16)

            def load_wq(h, b, source):
                sp.wait_ge(wq_lo_ready, blk(h, b) + START)
                sp.dma_start(wq_raw[:, :, :], wq_blocks[source]).then_inc(wq_in, 16)

            def load_w(h, pair):
                if not (isinstance(h, int) and h == pair == 0):
                    sp.wait_ge(w_lo_ready, proj(h, pair, 0, 0))
                for m in range(2):
                    sp.dma_start(w_raw[m][:, :, :, :], w_pairs[m][pair]).then_inc(w_in[m], 16)

            def load_adj(b, chunks):
                for k in chunks:
                    if not (isinstance(b, int) and b == 0 and k < 2):
                        sp.wait_ge(bias_added, b * 4 + (k - 1) + START)
                    sp.dma_start(adj_raw[k % 2][:, :], adj_chunks[b, CHUNKS[k][0], CHUNKS[k][1]]).then_inc(adj_in[k % 2], 16)

            def load_bias(h, b, pairs):
                for p in pairs:
                    if isinstance(h, int) and h == 0 and p == 0:
                        for u in range(2):
                            sp.wait_ge(bias_stored[u], (b + 1) * (H // 2) * 16)
                        sp.sem_inc(sp_met, 1)
                    if not (isinstance(h, int) and isinstance(b, int) and h == b == 0 and p < 2):
                        sp.wait_ge(logits_ready, unit(h, b, 2 * p - 2) + START)
                    sp.dma_start(bias[p % 2][:, :, :], bias_dram[b, 2 * p:2 * p + 2].rearrange(
                        "c p k s q -> p c (k s q)")).then_inc(bias_in[p % 2], 16)

            def head(h, first, last):
                if not first:
                    load_bias(h, 0, range(2))
                    for pair in range(2, PAIRS):
                        load_w(h, pair)
                    if not last:
                        load_x(h + 1)
                if not last and not first:
                    load_w(h + 1, 0)
                load_wq(h, 2, 2)
                load_bias(h, 0, range(2, PAIRS))
                if not last:
                    load_w(h + 1, 1)

                def block_of_queries(b, wq_source, wq_b, making):
                    if making:
                        load_adj(b + 1, range(2))
                    load_bias(h, b, range(2))
                    if wq_source is not None:
                        load_wq(h, wq_b, wq_source)
                    load_bias(h, b, range(2, PAIRS))
                    if making:
                        load_adj(b + 1, range(2, 4))

                with sp.Fori(1, H - 2) as b:
                    block_of_queries(b, b + 2, b + 2, first)
                block_of_queries(H - 2, None if last else 0, H, first)
                block_of_queries(H - 1, None if last else 1, H + 1, False)

            sp.dma_start(xrows[:, :, :], x_heads[0]).then_inc(xrows_in, 16)
            load_w(0, 0)
            sp.dma_start(wo_raw[:, :, :], wout_heads[0]).then_inc(wo_in, 16)
            sp.dma_start(wq_raw[:, :, :], wq_blocks[0]).then_inc(wq_in, 16)
            load_adj(0, range(2))
            load_w(0, 1)
            load_adj(0, range(2, 4))
            load_wq(0, 1, 1)
            if PAIRS > 2:
                load_w(0, 2)
            load_adj(1, range(2))
            for pair in range(3, PAIRS):
                load_w(0, pair)
            load_adj(1, range(2, 3))
            load_w(1, 0)
            load_adj(1, range(3, 4))
            for s in range(ST):
                sp.dma_start(acc[:, s], x_halves[s].rearrange("r (b e) -> r b e", b=H)).then_inc(acc_in, 16)
            load_bias(0, 0, range(2))
            load_x(1)
            heads(sp, head)
            for s in range(ST):
                sp.wait_ge(normed, H * (s + 1))
                sp.dma_start(out_halves[s], logits_sb[:, s * H // 2:(s + 1) * H // 2, :].rearrange("p c e -> p (c e)")).then_inc(stored, 16)
            sp.wait_ge(stored, 16 * ST)

        @block.gpsimd
        def _(pool):
            def cut_wq(h, b):
                pool.wait_ge(wq_hi_ready, blk(h, b, 1))
                pool.tensor_tensor(wq_lo[:, :, :], wq_raw[:, :, :], wq_hi[:, :, :],
                                   ALU.subtract).then_inc(wq_lo_ready, 1)

            def add_bias(b, k):
                pool.wait_ge(masked_ready, b * 4 + (k + 1))
                pool.tensor_tensor(masked[k % 2][:, :], adj_raw[k % 2][:, :], masked[k % 2][:, :], ALU.add).then_inc(bias_added, 1)

            def shift(h, b, c):
                if c == 0:
                    pool.wait_ge(maxes_ready, blk(h, b, 1) + START)
                if not (isinstance(h, int) and isinstance(b, int) and h == b == 0):
                    pool.wait_ge(pt_lo_ready, unit(h, b, c + 1 - H))
                pool.sem_inc(pool_met, 1)
                pool.tensor_tensor(prob[:, c, :], logits_sb[:, c, :], maxes[:, :, :].rearrange("p t q -> p (t q)"),
                                   ALU.subtract).then_inc(shifted, 1)

            def step(h, b, in_s, in_q, next_wq, first, last):
                for c in range(H):
                    if not (isinstance(h, int) and isinstance(b, int) and h == b == 0):
                        shift(h, b, c)
                    if first and c == H // 2:
                        add_bias(b + 2, 0)
                if first:
                    for k in range(1, 4):
                        add_bias(b + 2, k)
                if in_q == QUERIES and next_wq:
                    cut_wq(h, b + 3)

            for s in STARTED["pool"]:
                pool.sem_inc(s, START)
            pool.memset(ident[:, :], 0.0).then_inc(ident_zero, 1)
            pool.wait_ge(ident_zero, 1)
            pool.affine_select(out=ident[:, :], in_=ident[:, :], compare_op=ALU.not_equal, fill=1.0, base=0,
                               pattern=[[-1, P]], channel_multiplier=1).then_inc(ident_ready, 1)
            pool.memset(half_mask[:, :], 0.5 * MASKED).then_inc(half_mask_ready, 1)
            pool.memset(ones[:, :], 1.0).then_inc(ones_ready, 1)
            cut_wq(0, 0)
            for b in range(2):
                for k in range(4):
                    add_bias(b, k)
            cut_wq(0, 1)
            cut_wq(0, 2)

            def head(h, first, last):
                if not first:
                    cut_wq(h, 1)
                    cut_wq(h, 2)
                if first:
                    for c in range(H):
                        shift(0, 0, c)
                        if c == H // 2:
                            add_bias(2, 0)
                    for k in range(1, 4):
                        add_bias(2, k)
                    cut_wq(0, 3)
                    if H > 4:
                        with pool.Fori(1, H - 3) as b:
                            step(h, b, SCORES, QUERIES, True, first, last)
                    for b in range(max(H - 3, 1), H):
                        step(h, b, SCORES, QUERIES if b == H - 3 else NOTHING, True, b == H - 3, last)
                else:
                    steps(pool, h, first, last, step)

            heads(pool, head)

        @block.tensor
        def _(pe):
            def product(ps, lhs, rhs, tiles):
                terms = [(a, b, t) for t in range(tiles) for a, b in ((0, 0), (0, 1), (1, 0))]
                for i, (a, b, t) in enumerate(terms):
                    last = pe.matmul(ps, lhs(a, t), rhs(b, t), start=(i == 0), stop=(i == len(terms) - 1))
                return last

            def x_part(b, t):
                return (x_hi, x_lo)[b][:, t, :]

            def transpose_x(h):
                pe.wait_ge(xrows_in, (h + 1) * 16)
                for t in range(KT):
                    for s in range(ST):
                        last = pe.transpose(ps_s[0][:, t * R + s * P:t * R + (s + 1) * P],
                                            xrows[:, s, t * P:(t + 1) * P], ident[:, :])
                last.then_inc(xt_ps, 1)

            def project_kv(h, pair, m, u):
                pe.wait_ge(w_lo_ready, proj(h, pair, m, u) + 1)
                if m and isinstance(pair, int) and pair == LAST:
                    pe.wait_ge(logits_ready, unit(h, 0, H - RING + u) + 1 + START)
                for t in range(KT):
                    last = product(v_bank(pair, m, u)[:, t * R:(t + 1) * R],
                                   lambda a, k: (w_hi, w_lo)[a][m][u][:, k, t * P:(t + 1) * P], x_part, KT)
                last.then_inc(kv_ps, 1)

            def project_vout(h, pair, u):
                if isinstance(pair, int) and pair == u == 0:
                    pe.wait_ge(out_added, blk(h, 0) * ST + START)
                    pe.wait_ge(xw_lo, h * 2 + 2 + START)
                pe.wait_ge(kv_lo, proj(h, pair, 1, u) + 1)
                if u == 0:
                    pe.wait_ge(vp_lo, blk(h, pair * 2) + START)
                if isinstance(pair, int) and pair == LAST - 1 and u == 0:
                    pe.wait_ge(q_lo_ready, blk(h, 0, 1))
                for s in range(ST):
                    last = product(ps_o[u][:, s * d:(s + 1) * d],
                                   lambda a, k: (vt_hi, vt_lo)[a][u][:, k, s * P:(s + 1) * P],
                                   lambda b, k: (wo_hi, wo_lo)[b][:, k, :], KT)
                last.then_inc(vp_ps, 1)

            def project_q(h, b, ps):
                pe.wait_ge(wq_lo_ready, blk(h, b, 1) + START)
                for t in range(KT):
                    last = product(ps[:, t * R:(t + 1) * R],
                                   lambda a, k: (wq_hi, wq_lo)[a][:, k, t * P:(t + 1) * P], x_part, KT)
                last.then_inc(q_ps, 1)

            def scores(c):
                for t in range(ST):
                    last = product(ps_s[c % RING][:, t * R:(t + 1) * R],
                                   lambda a, k: (k_hi, k_lo)[a][:, k, c * R + t * P:c * R + (t + 1) * P],
                                   lambda b, k: (q_hi, q_lo)[b][:, k, :], KT)
                last.then_inc(scores_ps, 1)

            def weigh_values(h, b, c):
                if c == 0:
                    pe.wait_ge(out_added, blk(h, b) * ST + START)
                    pe.wait_ge(vp_lo, blk(h, H) + START)
                pe.wait_ge(pt_lo_ready, unit(h, b, c) + 1)
                for s in range(ST):
                    for t in range(ST):
                        k = c * ST + t
                        hi, lo = (part[c % 2][:, t * R + s * P:t * R + (s + 1) * P] for part in (pt_hi, pt_lo))
                        pe.matmul(ps_o[s][:, 0:d + ONES], hi, v_hi[:, k, :], start=(k == 0), stop=False)
                        pe.matmul(ps_o[s][:, 0:d], hi, v_lo[:, k, :], start=False, stop=False)
                        last = pe.matmul(ps_o[s][:, 0:d + ONES], lo, v_hi[:, k, :], start=False, stop=(k == JT - 1))
                last.then_inc(pv_done, 1)

            def maxes_of(what, h, b):
                if what == "MT":
                    pe.wait_ge(keymax_ready, unit(h, b, H))
                    for s in range(ST):
                        last = pe.transpose(ps_m[:, s * P:(s + 1) * P], keymax[:, s * P:(s + 1) * P], ident[:, :])
                    last.then_inc(keymax_ps, 1)
                else:
                    pe.wait_ge(maxes_ready, blk(h, b) + START)
                    pe.wait_ge(rowmax_ready, blk(h, b, 1))
                    for s in range(ST):
                        last = pe.transpose(ps_m[:, R + s * P:R + (s + 1) * P],
                                            rowmax[:, s:s + 1].to_broadcast([P, P]), ident[:, :])
                    last.then_inc(maxes_ps, 1)

            def transpose_bias(b, i):
                k, c0 = group_chunk(i)
                pe.wait_ge(bias_cut, b * H + i + START)
                pe.wait_ge(bias_added, b * 4 + (k + 1) + START)
                for j in range(4):
                    last = pe.transpose(ps_b[:, j * P:(j + 1) * P],
                                        masked[k % 2][:, :].rearrange("p (k c) -> p c k", c=H)[:, c0 + j, :], ident[:, :])
                last.then_inc(bias_ps, 1)

            def step(h, b, in_s, in_q, next_wq, first, last):
                for what, c in ORDER:
                    if what == "PV":
                        weigh_values(h, b, c)
                    elif what in ("MT", "MB") and in_s == SCORES:
                        maxes_of(what, h, b + 1)
                    elif what == "S" and in_s == SCORES:
                        if c == 0:
                            pe.wait_ge(q_lo_ready, blk(h, b, 2))
                        pe.wait_ge(logits_ready, unit(h, b + 1, c - RING) + 1 + START)
                        scores(c)
                    elif what == "S" and in_s == NEXT_KV:
                        for m, u in KV[c:c + 1]:
                            if m == u == 0:
                                pe.wait_ge(xw_lo, h * 2 + 3 + START)
                                pe.wait_ge(logits_ready, unit(h, H, 0) + START)
                            project_kv(h + 1, 0, m, u)
                    elif what == "Q" and in_q != NOTHING:
                        pe.wait_ge(logits_ready, unit(h, b + 1, H - RING) + 1 + START)
                        if in_q == QUERIES:
                            project_q(h, b + 2, ps_s[0])
                        else:
                            transpose_x(h + 1)
                    if first and (what, c) in BIAS_AT:
                        transpose_bias(b + 2, BIAS_AT.index((what, c)))

            def head(h, first, last):
                def queries(h, b):
                    if b == 0:
                        pe.wait_ge(out_added, blk(h, 0) * ST + START)
                        pe.wait_ge(vp_lo, blk(h, 2 * LAST - 2) + START)
                        project_q(h, 0, ps_o[0])
                    else:
                        pe.wait_ge(logits_ready, unit(h, 0, H - 2) + 1 + START)
                        project_q(h, 1, ps_s[2])

                def first_scores(h, b, c):
                    if c < 2:
                        pe.wait_ge(kv_lo, proj(h, LAST, 0, c) + 1)
                    if c >= RING:
                        pe.wait_ge(logits_ready, unit(h, 0, c - RING) + 1 + START)
                    scores(c)

                phase_a(pe, h, first, project_vout, project_kv, queries, first_scores, maxes_of,
                        spares(lambda i: transpose_bias(i // H, i % H)) if first else lambda: None)
                steps(pe, h, first, last, step)

            for s in STARTED["pe"]:
                pe.sem_inc(s, START)
            pe.wait_ge(ident_ready, 1)
            transpose_x(0)
            pe.wait_ge(xw_lo, 1 + START)
            for m, u in KV:
                project_kv(0, 0, m, u)
            heads(pe, head)

        @block.scalar
        def _(act):
            def cut_weight(h, pair, m, u):
                act.wait_ge(w_in[m], (h * PAIRS + pair + 1) * 16)
                act.activation(w_hi[m][u][:, :, :], w_raw[m][:, :, u, :], ACT.Copy).then_inc(w_hi_ready, 1)

            def cut_wq(h, b):
                act.wait_ge(wq_in, blk(h, b, 1) * 16)
                act.wait_ge(q_ps, blk(h, b) + START)
                act.activation(wq_hi[:, :, :], wq_raw[:, :, :], ACT.Copy).then_inc(wq_hi_ready, 1)

            def cut_x(h):
                act.wait_ge(xt_ps, h + 1 + START)
                act.activation(x_hi[:, :, :], halves(ps_s[0]), ACT.Copy).then_inc(xw_hi, 1)

            def cut_wout(h):
                act.wait_ge(wo_in, (h + 1) * 16)
                act.activation(wo_hi[:, :, :], wo_raw[:, :, :], ACT.Copy).then_inc(xw_hi, 1)

            def cut_kv(h, pair, m, u, next_pair, last=False):
                act.wait_ge(kv_ps, proj(h, pair, m, u) + 1)
                dst = vt_hi[u][:, :, :] if m else k_hi[:, :, bass.ds((pair * 2 + u) * R, R)]
                act.activation(dst, halves(v_bank(pair, m, u)), ACT.Copy).then_inc(kv_hi, 1)
                if not last:
                    cut_weight(h, next_pair, m, u)

            def cut_vout(h, pair, u):
                act.wait_ge(vp_ps, blk(h, pair * 2, u + 1))
                act.activation(v_hi[:, bass.ds((pair * 2 + u) * ST, ST), 0:d], halves(ps_o[u]), ACT.Copy).then_inc(vp_hi, 1)

            def cut_q(h, b, ps):
                act.wait_ge(q_ps, blk(h, b, 1) + START)
                act.activation(q_hi[:, :, :], halves(ps), ACT.Copy, scale=QSCALE).then_inc(q_hi_ready, 1)

            def exps(h, b, c):
                act.wait_ge(shifted, unit(h, b, c) + 1)
                act.activation(prob[:, c, :], prob[:, c, :], ACT.Exp, scale=2.0).then_inc(exp_ready, 1)

            def cut_exps(h, b, c):
                act.wait_ge(exp_ready, unit(h, b, c) + 1)
                act.wait_ge(pv_done, unit(h, b, c) - 1 + START)
                act.activation(pt_hi[c % 2][:, :], prob[:, c, :], ACT.Copy).then_inc(pt_hi_ready, 1)

            def copy_maxes(what, h, b):
                if what == "MB":
                    if not (isinstance(h, int) and isinstance(b, int) and h == b == 0):
                        act.wait_ge(shifted, unit(h, b, 0))
                    act.wait_ge(maxes_ps, blk(h, b, 1))
                    act.activation(maxes[:, :, :], ps_m[:, R:2 * R].unsqueeze(1).to_broadcast([P, 2, R]),
                                   ACT.Copy).then_inc(maxes_ready, 1)

            def store_bias(b, i):
                k, c0 = group_chunk(i)
                s, g = CHUNKS[k]
                if not (isinstance(b, int) and b == 0 and i < 2):
                    act.wait_ge(bias_stored[i % 2], (b * (H // 2) + i // 2) * 16)
                act.wait_ge(bias_ps, b * H + i + 1)
                act.activation(bias_t[i % 2][:, :], ps_b[:, :], ACT.Copy).then_inc(bias_cut, 1)
                act.wait_ge(bias_cut, b * H + i + 1 + START)
                act.dma_start(bias_dram[b, c0:c0 + 4, :, g, s, :].rearrange("c p q -> p c q"),
                              bias_t[i % 2][:, :].rearrange("p (c q) -> p c q", c=4)).then_inc(bias_stored[i % 2], 16)

            def step(h, b, in_s, in_q, next_wq, first, last):
                exps(h, b, 0)
                cut_exps(h, b, 0)
                for what, c in ORDER:
                    if (what, c) in CUT_AT:
                        cut_exps(h, b, CUT_AT[what, c])
                    if what == "MB" and in_s == SCORES:
                        copy_maxes(what, h, b + 1)
                    if what == "S" and c + 1 < H:
                        exps(h, b, c + 1)
                    if what == "S" and in_s == NEXT_KV:
                        for m, u in KV[c:c + 1]:
                            cut_kv(h + 1, 0, m, u, 1)
                    elif what == "Q" and in_q == QUERIES:
                        cut_q(h, b + 2, ps_s[0])
                    elif (what, c) == ("PV", H - 4) and in_q == QUERIES and next_wq:
                        cut_wq(h, b + 3)
                    elif what == "Q" and in_q == NEXT_X:
                        cut_x(h + 1)
                        cut_wout(h + 1)
                    if first and (what, c) in BIAS_AT:
                        store_bias(b + 2, BIAS_AT.index((what, c)))

            def head(h, first, last):
                def kv(h, pair, m, u):
                    if isinstance(pair, int) and pair == LAST:
                        cut_kv(h, LAST, m, u, 0, True)
                        if not last:
                            cut_weight(h + 1, 0, m, u)
                    else:
                        cut_kv(h, pair, m, u, pair + 1)

                def queries(h, b):
                    cut_q(h, b, ps_s[2] if b else ps_o[0])
                    cut_wq(h, b + 1)

                phase_a(act, h, first, cut_vout, kv, queries, lambda h, b, c: None, copy_maxes,
                        spares(lambda i: store_bias(i // H, i % H)) if first else lambda: None)
                steps(act, h, first, last, step)

            for s in STARTED["act"]:
                act.sem_inc(s, START)
            cut_x(0)
            for m, u in KV:
                cut_weight(0, 0, m, u)
            cut_wout(0)
            cut_wq(0, 0)
            act.wait_ge(ones_ready, 1)
            act.activation(v_hi[:, :, d:d + ONES], ones[:, 0:1].to_broadcast([P, JT * ONES]).rearrange("p (j o) -> p j o", j=JT),
                           ACT.Copy)
            for m, u in KV:
                cut_kv(0, 0, m, u, 1)
            heads(act, head)
            act.wait_ge(veps_ready, 1)
            act.activation(std[:, :, :], veps[:, :, :], ACT.Sqrt).then_inc(std_ready, 1)

        @block.vector
        def _(dve):
            def cut_weight(h, pair, m, u):
                dve.wait_ge(w_hi_ready, proj(h, pair, m, u) + 1)
                dve.tensor_tensor(w_lo[m][u][:, :, :], w_raw[m][:, :, u, :], w_hi[m][u][:, :, :],
                                  ALU.subtract).then_inc(w_lo_ready, 1)

            def cut_x(h):
                dve.wait_ge(xw_hi, h * 2 + 1)
                dve.tensor_tensor(x_lo[:, :, :], halves(ps_s[0]), x_hi[:, :, :], ALU.subtract).then_inc(xw_lo, 1)

            def cut_wout(h):
                dve.wait_ge(xw_hi, h * 2 + 2)
                dve.tensor_tensor(wo_lo[:, :, :], wo_raw[:, :, :], wo_hi[:, :, :], ALU.subtract).then_inc(xw_lo, 1)

            def cut_kv(h, pair, m, u, next_pair, last=False):
                dve.wait_ge(kv_hi, proj(h, pair, m, u) + 1)
                cols = bass.ds((pair * 2 + u) * R, R)
                hi, dst = ((vt_hi[u][:, :, :], vt_lo[u][:, :, :]) if m else (k_hi[:, :, cols], k_lo[:, :, cols]))
                dve.tensor_tensor(dst, halves(v_bank(pair, m, u)), hi, ALU.subtract).then_inc(kv_lo, 1)
                if not last:
                    cut_weight(h, next_pair, m, u)

            def cut_vout(h, pair, u):
                dve.wait_ge(vp_hi, blk(h, pair * 2, u + 1))
                tiles = bass.ds((pair * 2 + u) * ST, ST)
                dve.tensor_tensor(v_lo[:, tiles, :], halves(ps_o[u]), v_hi[:, tiles, 0:d], ALU.subtract).then_inc(vp_lo, 1)

            def cut_q(h, b, ps):
                dve.wait_ge(q_hi_ready, blk(h, b, 1))
                dve.scalar_tensor_tensor(q_lo[:, :, :], halves(ps), QSCALE, q_hi[:, :, :],
                                         ALU.mult, ALU.subtract).then_inc(q_lo_ready, 1)

            def cut_exps(h, b, c):
                dve.wait_ge(pt_hi_ready, unit(h, b, c) + 1)
                dve.tensor_tensor(pt_lo[c % 2][:, :], prob[:, c, :], pt_hi[c % 2][:, :], ALU.subtract).then_inc(pt_lo_ready, 1)

            def mask(b, k):
                s, g = CHUNKS[k]
                dve.wait_ge(adj_in[k % 2], (b * 2 + k // 2 + 1) * 16)
                if not (isinstance(b, int) and b == 0 and k < 2):
                    dve.wait_ge(bias_ps, b * H + (k - 1) * QUADS)
                if g == 0:
                    dve.wait_ge(keep_steps, b * 4 + 2 * s + START)
                dve.scalar_tensor_tensor(masked[k % 2][:, :], adj_raw[k % 2][:, :], 0.0,
                                         half_mask[:, 0:1].to_broadcast([P, CHUNK]), ALU.is_equal, ALU.mult,
                                         accum_out=mask_sum[:, g:g + 1]).then_inc(masked_ready, 1)
                if g == ST - 1:
                    dve.wait_ge(masked_ready, b * 4 + (k + 1))
                    dve.tensor_reduce(mask_max[:, :], mask_sum[:, :], AX.X, ALU.max).then_inc(keep_steps, 1)
                    dve.wait_ge(keep_steps, b * 4 + (2 * s + 1) + START)
                    dve.tensor_scalar(keep[:, s, bass.ds(b, 1)], mask_max[:, :], 0.5 * MASKED * CHUNK, None,
                                      ALU.is_gt).then_inc(keep_steps, 1)

            def logits(h, b, c):
                if c % 2 == 0:
                    p = c // 2
                    dve.wait_ge(bias_in[p % 2], (blk(h, b) * (H // 4) + (p // 2 + 1)) * 16)
                if not (isinstance(h, int) and isinstance(b, int) and h == b == 0):
                    dve.wait_ge(shifted, unit(h, b, c + 1 - H))
                dve.wait_ge(scores_ps, unit(h, b, c) + 1)
                dve.tensor_tensor(logits_sb[:, c, :], ps_s[c % RING][:, :], bias[c // 2 % 2][:, c % 2, :],
                                  ALU.add).then_inc(logits_ready, 1)
                if c == 1:
                    if not (isinstance(h, int) and isinstance(b, int) and h == b == 0):
                        dve.wait_ge(keymax_ps, blk(h, b))
                elif c > 1:
                    dve.wait_ge(keymax_ready, unit(h, b, c - 1))
                if c:
                    dve.wait_ge(logits_ready, unit(h, b, c + 1) + START)
                    dve.tensor_tensor(keymax[:, :], logits_sb[:, c, :], logits_sb[:, 0, :] if c == 1 else keymax[:, :],
                                      ALU.max).then_inc(keymax_ready, 1)
                if c == H - 1:
                    dve.wait_ge(keymax_ready, unit(h, b, c))
                    dve.tensor_tensor(keymax[:, 0:R], keymax[:, 0:R], keymax[:, R:2 * R], ALU.max).then_inc(keymax_ready, 1)

            def reduce_maxes(what, h, b):
                if what == "MT":
                    dve.wait_ge(keymax_ps, blk(h, b, 1))
                    dve.tensor_reduce(rowmax[:, :], ps_m[:, 0:R].rearrange("p (s k) -> p s k", s=ST), AX.X,
                                      ALU.max).then_inc(rowmax_ready, 1)

            def add_tiles(h, b):
                dve.wait_ge(pv_done, unit(h, b, H) + START)
                for s in range(ST):
                    dve.reciprocal(rdenom[:, s:s + 1], ps_o[s][:, d:d + 1]).then_inc(rdenom_ready, 1)
                for s in range(ST):
                    dve.wait_ge(rdenom_ready, blk(h, b) * ST + s + 1)
                    dve.tensor_tensor(weight[:, s:s + 1], rdenom[:, s:s + 1], keep[:, s, bass.ds(b, 1)],
                                      ALU.mult).then_inc(weight_ready, 1)
                for s in range(ST):
                    dve.wait_ge(weight_ready, blk(h, b) * ST + s + 1)
                    a = acc[:, s, b, :]
                    dve.scalar_tensor_tensor(a, ps_o[s][:, 0:d], weight[:, s:s + 1], a,
                                             ALU.mult, ALU.add).then_inc(out_added, 1)

            def row_stats(b):
                for s in range(ST):
                    dve.wait_ge(out_added, blk(H - 1, b) * ST + (s + 1) + START)
                    dve.bn_stats(stats[:, s, b, :], acc[:, s, b, :]).then_inc(stats_ready, 1)

            def step(h, b, in_s, in_q, next_wq, first, last):
                cut_exps(h, b, 0)
                for what, c in ORDER:
                    if what == "MT" and in_s == SCORES:
                        reduce_maxes(what, h, b + 1)
                    if (what, c) in CUT_AT:
                        cut_exps(h, b, CUT_AT[what, c])
                    if what == "S" and in_s == SCORES:
                        logits(h, b + 1, c)
                    elif what == "S" and in_s == NEXT_KV:
                        for m, u in KV[c:c + 1]:
                            cut_kv(h + 1, 0, m, u, 1)
                    elif what == "Q" and in_q == QUERIES:
                        cut_q(h, b + 2, ps_s[0])
                    elif what == "Q" and in_q == NEXT_X:
                        cut_x(h + 1)
                        cut_wout(h + 1)
                    if first:
                        for k in range(4):
                            if MASK_AT[k] == (what, c):
                                mask(b + 2, k)
                add_tiles(h, b)
                if last:
                    row_stats(b)

            def head(h, first, last):
                def kv(h, pair, m, u):
                    if isinstance(pair, int) and pair == LAST:
                        cut_kv(h, LAST, m, u, 0, True)
                        if not last:
                            cut_weight(h + 1, 0, m, u)
                    else:
                        cut_kv(h, pair, m, u, pair + 1)

                def mask_after(i):
                    k = (i + 1) // QUADS + 1
                    if (i + 1) % QUADS == 0 and k < 8:
                        mask(k // 4, k % 4)

                phase_a(dve, h, first, cut_vout, kv, lambda h, b: cut_q(h, b, ps_s[2] if b else ps_o[0]), logits,
                        reduce_maxes, spares(mask_after) if first else lambda: None)
                if first:
                    dve.wait_ge(acc_in, 16 * ST)
                steps(dve, h, first, last, step)

            for s in STARTED["dve"]:
                dve.sem_inc(s, START)
            dve.wait_ge(half_mask_ready, 1)
            cut_x(0)
            for m, u in KV:
                cut_weight(0, 0, m, u)
            cut_wout(0)
            for m, u in KV:
                cut_kv(0, 0, m, u, 1)
                if u == 1:
                    mask(0, m)
            heads(dve, head)

            tiles = [(s, b) for s in range(ST) for b in range(H)]
            dve.wait_ge(stats_ready, JT)
            for s, b in tiles:
                dve.bn_aggr(moments[:, s, b, :], stats[:, s, b, :]).then_inc(moments_ready, 1)
            dve.wait_ge(moments_ready, JT)
            dve.tensor_scalar(veps[:, :, :], moments[:, :, :, 1], EPS, None, ALU.add).then_inc(veps_ready, 1)
            dve.wait_ge(std_ready, 1)
            dve.reciprocal(rstd[:, :, :], std[:, :, :]).then_inc(rstd_ready, 1)
            dve.wait_ge(rstd_ready, 1)
            for s, b in tiles:
                place = s * H + b
                dve.tensor_scalar(logits_sb[:, place // 2, place % 2 * d:(place % 2 + 1) * d], acc[:, s, b, :],
                                  moments[:, s, b, 0:1], rstd[:, s, b:b + 1], ALU.subtract, ALU.mult).then_inc(normed, 1)


_INPUTS = ["x", "adj", "L0_gnn_Wq", "L0_gnn_Wk", "L0_gnn_Wv", "L0_gnn_Wout"]


def kernel(**inputs):
    import numpy as np
    import concourse.bacc as bacc
    from concourse.bass_utils import run_bass_kernel_spmd

    nc = bacc.Bacc("TRN2", target_bir_lowering=False, num_devices=1)
    arrays, args = {}, []
    for name in _INPUTS:
        a = np.ascontiguousarray(inputs[name])
        arrays[f"in_{name}"] = a
        args.append(nc.dram_tensor(f"in_{name}", a.shape, mybir.dt.from_np(a.dtype), kind="ExternalInput").ap())
    out = nc.dram_tensor("out", arrays["in_x"].shape, F32, kind="ExternalOutput").ap()
    attention_layer_norm(nc, *args, out)
    r = run_bass_kernel_spmd(nc, [arrays], core_ids=[0])
    return r.results[0]["out"]
```

```python
from contextlib import ExitStack

import concourse.bass as bass
from concourse import mybir

F32 = mybir.dt.float32
F32R = mybir.dt.float32r
ALU = mybir.AluOpType
ACT = mybir.ActivationFunctionType
AX = mybir.AxisListType

P = 128
BANK = 512
MASKED = -1000000.0
EPS = 1e-5


def attention_layer_norm(nc, x, adj, wq, wk, wv, wout, out):
    n, d = x.shape
    H = wq.shape[1] // d
    R = n // H
    KT = d // P
    ST = R // P
    JT = n // P
    CHUNK = P * H
    QUADS = H // 4
    RING = 4
    ONES = 2
    QSCALE = 0.5 * float(d) ** -0.5
    assert KT == 2 and ST == 2 and ST * R == BANK and KT * d == BANK and H == 8

    adj_chunks = adj.rearrange("(s r b) (g j) -> b s g r j", s=ST, r=P, b=H, g=ST)
    x_halves = x.rearrange("(s r b) e -> s r (b e)", s=ST, r=P, b=H)
    out_halves = out.rearrange("(s r b) e -> s r (b e)", s=ST, r=P, b=H)
    x_heads = x.rearrange("(h s p) e -> h p s e", h=H, s=ST)
    w_pairs = [w.rearrange("(t p) (c u e) -> c p t u e", t=KT, u=2, e=d) for w in (wk, wv)]
    wq_blocks = wq.rearrange("(t p) (c e) -> c p t e", t=KT, c=H)
    wout_heads = wout.rearrange("(h t p) e -> h p t e", h=H, t=KT)

    ctx = ExitStack()
    with ctx:
        def sb(name, shape, dt=F32):
            return ctx.enter_context(nc.sbuf_tensor(name, shape, dt))

        def sem(name):
            return ctx.enter_context(nc.semaphore(name))

        bias_dram = nc.dram_tensor("bias_scratch", [H, H, P, ST, ST, P], F32, kind="Internal").ap()

        ident = sb("ident", [P, P])
        wq_raw = sb("wq_raw", [P, KT, d])
        w_raw = [sb(f"w_raw{m}", [P, KT, 2, d]) for m in range(2)]
        wo_raw = sb("wo_raw", [P, KT, d])
        xrows = sb("xrows", [P, ST, d])
        x_hi, x_lo = sb("x_hi", [P, KT, R], F32R), sb("x_lo", [P, KT, R], F32R)
        wo_hi, wo_lo = sb("wo_hi", [P, KT, d], F32R), sb("wo_lo", [P, KT, d], F32R)
        wq_hi, wq_lo = sb("wq_hi", [P, KT, d], F32R), sb("wq_lo", [P, KT, d], F32R)
        w_hi = [[sb(f"w_hi{m}{u}", [P, KT, d], F32R) for u in range(2)] for m in range(2)]
        w_lo = [[sb(f"w_lo{m}{u}", [P, KT, d], F32R) for u in range(2)] for m in range(2)]
        vt_hi = [sb(f"vt_hi{u}", [P, KT, R], F32R) for u in range(2)]
        vt_lo = [sb(f"vt_lo{u}", [P, KT, R], F32R) for u in range(2)]
        q_hi, q_lo = sb("q_hi", [P, KT, R], F32R), sb("q_lo", [P, KT, R], F32R)
        k_hi, k_lo = sb("k_hi", [P, KT, n], F32R), sb("k_lo", [P, KT, n], F32R)
        v_hi = sb("v_hi", [P, JT, d + ONES], F32R)
        v_lo = sb("v_lo", [P, JT, d], F32R)
        adj_raw = [sb(f"adj_raw{u}", [P, CHUNK]) for u in range(2)]
        masked = [sb(f"masked{u}", [P, CHUNK]) for u in range(2)]
        half_mask, ones = sb("half_mask", [P, 1]), sb("ones", [P, 1])
        bias_t = [sb(f"bias_t{u}", [P, BANK]) for u in range(2)]
        bias = [sb(f"bias{u}", [P, 2, BANK]) for u in range(2)]
        logits_sb = sb("logits", [P, H, BANK])
        prob = sb("prob", [P, H, BANK])
        pt_hi = [sb(f"pt_hi{u}", [P, BANK], F32R) for u in range(2)]
        pt_lo = [sb(f"pt_lo{u}", [P, BANK], F32R) for u in range(2)]
        acc = sb("acc", [P, ST, H, d])
        keymax = sb("keymax", [P, BANK])
        rowmax = sb("rowmax", [P, ST])
        maxes = sb("maxes", [P, 2, R])
        rdenom, weight = sb("rdenom", [P, ST]), sb("weight", [P, ST])
        mask_sum = sb("mask_sum", [P, ST])
        mask_max = sb("mask_max", [P, 1])
        keep = sb("keep", [P, ST, H])
        stats = sb("stats", [P, ST, H, 6])
        moments = sb("moments", [P, ST, H, 2])
        veps, std, rstd, norm_bias = (sb(name, [P, ST, H]) for name in ("veps", "std", "rstd", "norm_bias"))

        def bank(name):
            return ctx.enter_context(nc.psum_tensor(name, [P, BANK], F32))

        ps_s = [bank(f"ps_s{c}") for c in range(RING)]
        ps_o = [bank(f"ps_o{u}") for u in range(2)]
        ps_m = bank("ps_m")
        ps_b = bank("ps_b")

        ident_zero, ident_ready, half_mask_ready = sem("ident_zero"), sem("ident_ready"), sem("half_mask_ready")
        ones_ready = sem("ones_ready")
        w_in = [sem(f"w_in{m}") for m in range(2)]
        w_early_in = [sem(f"w_early_in{i}") for i in range(3)]
        acc_in, wq_in, xrows_in, wo_in = sem("acc_in"), sem("wq_in"), sem("xrows_in"), sem("wo_in")
        adj_in = [sem(f"adj_in{u}") for u in range(2)]
        masked_ready, bias_added = sem("masked_ready"), sem("bias_added")
        bias_ps, bias_cut = sem("bias_ps"), sem("bias_cut")
        keep_steps = sem("keep_steps")
        bias_stored = [sem(f"bias_stored{u}") for u in range(2)]
        bias_in = [sem(f"bias_in{u}") for u in range(2)]
        xt_ps, xw_hi, xw_lo = sem("xt_ps"), sem("xw_hi"), sem("xw_lo")
        w_hi_ready, w_lo_ready = sem("w_hi_ready"), sem("w_lo_ready")
        kv_ps, kv_hi, kv_lo = sem("kv_ps"), sem("kv_hi"), sem("kv_lo")
        vp_ps, vp_hi, vp_lo = sem("vp_ps"), sem("vp_hi"), sem("vp_lo")
        wq_hi_ready, wq_lo_ready = sem("wq_hi_ready"), sem("wq_lo_ready")
        q_ps, q_hi_ready, q_lo_ready = sem("q_ps"), sem("q_hi_ready"), sem("q_lo_ready")
        scores_ps, logits_ready, keymax_ready = sem("scores_ps"), sem("logits_ready"), sem("keymax_ready")
        keymax_ps, rowmax_ready, maxes_ps, maxes_ready = (
            sem("keymax_ps"), sem("rowmax_ready"), sem("maxes_ps"), sem("maxes_ready"))
        shifted, exp_ready = sem("shifted"), sem("exp_ready")
        pt_hi_ready, pt_lo_ready = sem("pt_hi_ready"), sem("pt_lo_ready")
        pv_done = sem("pv_done")
        rdenom_ready, weight_ready = sem("rdenom_ready"), sem("weight_ready")
        out_added = sem("out_added")
        stats_ready, moments_ready = sem("stats_ready"), sem("moments_ready")
        veps_ready, std_ready, rstd_ready, norm_bias_ready = (
            sem("veps_ready"), sem("std_ready"), sem("rstd_ready"), sem("norm_bias_ready"))
        normed = [sem(f"normed{s}") for s in range(ST)]
        stored = sem("stored")
        sp_met, pool_met = sem("sp_met"), sem("pool_met")
        START = 2
        STARTED = {"pe": (xt_ps, q_ps, pv_done), "pool": (wq_lo_ready, bias_added),
                   "act": (maxes_ready, bias_cut),
                   "dve": (keep_steps, xw_lo, vp_lo, logits_ready, out_added)}

        block = ctx.enter_context(nc.Block())

        def unit(h, b, c):
            return h * (H * H) + b * H + c

        def blk(h, c, u=0):
            return h * H + c + u

        def proj(h, pair, m, u):
            return h * (2 * H) + pair * 4 + (2 * m + u)

        PAIRS = H // 2
        LAST = PAIRS - 1
        KV = [(m, u) for m in range(2) for u in range(2)]
        LAG = 4
        ORDER = [("S", 0), ("S", 1)]
        for c in range(2, H):
            ORDER += [("PV", c - 2)] * (c - 2 < H - LAG) + [("S", c)]
        ORDER += [("Q", 0), ("PV", H - 4), ("MT", 0), ("PV", H - 3), ("MB", 0), ("PV", H - 2), ("PV", H - 1)]
        CUT_AT = {("S", 1): 1} | {ORDER[ORDER.index(("PV", c - 2)) + 1]: c for c in range(2, H)}
        BIAS_AT = [("S", 3), ("PV", 2), ("PV", 3), ("S", 5), ("S", 6), ("S", 7), ("Q", 0), ("PV", 4)]
        MASK_AT = {("S", 4): 2, ("S", 6): 3}
        NORM_PARTS = (slice(0, H - 1), slice(H - 1, H))
        SCORES, NEXT_KV, NOTHING, QUERIES, NEXT_X = "scores", "next kv", "nothing", "queries", "next x"
        CHUNKS = [(s, g) for s in range(ST) for g in range(ST)]

        def halves(ps):
            return ps[:, 0:KT * R].rearrange("p (t s) -> p t s", t=2)

        def steps(engine, h, first, last, step):
            with engine.Fori(0, H - 3) as b:
                step(h, b, SCORES, QUERIES, True, first, last)
            step(h, H - 3, SCORES, QUERIES, not last, first, last)
            step(h, H - 2, SCORES, NOTHING if last else NEXT_X, False, False, last)
            step(h, H - 1, NOTHING if last else NEXT_KV, NOTHING, False, False, last)

        def heads(engine, head):
            head(0, True, False)
            with engine.Fori(1, H - 1) as h:
                head(h, False, False)
            head(H - 1, False, True)

        def phase_a(engine, h, first, v_out, kv, queries, scores, maxes, spare, maxes_early=False):
            def pair_of_blocks(pair):
                for u in range(2):
                    kv(h, pair, 0, u)
                    spare()
                for u in range(2):
                    v_out(h, pair - 1, u)
                    spare()
                for u in range(2):
                    kv(h, pair, 1, u)
                    spare()

            if first:
                for pair in range(1, LAST):
                    pair_of_blocks(pair)
            else:
                pair_of_blocks(1)
                with engine.Fori(2, LAST) as pair:
                    pair_of_blocks(pair)
            queries(h, 0)
            spare()
            for u in range(2):
                kv(h, LAST, 0, u)
                spare()
            for u in range(2):
                v_out(h, LAST - 1, u)
                spare()
            for c in range(H):
                scores(h, 0, c)
                spare()
            kv(h, LAST, 1, 0)
            if maxes_early:
                maxes("MT", h, 0)
            kv(h, LAST, 1, 1)
            if not maxes_early:
                maxes("MT", h, 0)
            queries(h, 1)
            maxes("MB", h, 0)
            v_out(h, LAST, 0)
            v_out(h, LAST, 1)

        def v_bank(pair, m, u):
            return ps_s[u] if isinstance(pair, int) and pair == LAST else ps_s[2 * m + u]

        def spares(do):
            places = list(range(2 * H + 2))
            return lambda: places and do(places.pop(0))

        def bias_groups(do):
            return lambda e: do((e - 2) // H, (e - 2) % H) if e >= 2 else None

        def masked_chunk(b, k):
            if isinstance(b, int) and b == 0:
                return logits_sb[:, 2 * k:2 * k + 2, :].rearrange("p c e -> p (c e)")
            return masked[k % 2][:, :]

        def group_chunk(i):
            return i // QUADS, i % QUADS * 4

        def loaded_early(h, pair):
            early = [(0, 1), (0, 2), (1, 0)]
            return early.index((h, pair)) if isinstance(h, int) and isinstance(pair, int) and (h, pair) in early else None

        def weights_buffer(h, pair, m, u=None):
            i = loaded_early(h, pair)
            if i is None:
                both = w_raw[m][:, :, :, :]
            else:
                place = i % 2 * 4 + 2 * m
                both = prob[:, place:place + 2, :].rearrange("p t (u e) -> p t u e", u=2)
            return both if u is None else both[:, :, u, :]

        def weights_loaded(h, pair, m):
            i = loaded_early(h, pair)
            if i is not None:
                return w_early_in[i], 16 * 2
            if isinstance(h, int) and h == 0:
                return w_in[m], 16 * (1 if pair == 0 else 2)
            return w_in[m], 16 * (h * PAIRS + pair + 1 - 3)

        @block.sync
        def _(sp):
            def load_x(h):
                sp.wait_ge(xt_ps, h + START)
                sp.dma_start(xrows[:, :, :], x_heads[h]).then_inc(xrows_in, 16)
                sp.wait_ge(xw_lo, h * 2 + START)
                sp.dma_start(wo_raw[:, :, :], wout_heads[h]).then_inc(wo_in, 16)

            def load_wq(h, b, source):
                sp.wait_ge(wq_lo_ready, blk(h, b) + START)
                sp.dma_start(wq_raw[:, :, :], wq_blocks[source]).then_inc(wq_in, 16)

            def load_w(h, pair):
                for m in range(2):
                    if loaded_early(h, pair) == 2:
                        sp.wait_ge(w_lo_ready, proj(0, 1, m, 0) + 2)
                    elif isinstance(h, int) and h == 0:
                        if pair == LAST:
                            sp.wait_ge(w_lo_ready, proj(0, 0, m, 0) + 2)
                    else:
                        sp.wait_ge(w_lo_ready, proj(h, pair, m, 0) - 2)
                    sp.dma_start(weights_buffer(h, pair, m), w_pairs[m][pair]).then_inc(weights_loaded(h, pair, m)[0], 16)

            def load_adj(b, chunks):
                for k in chunks:
                    if not (isinstance(b, int) and b == 0 and k < 2):
                        sp.wait_ge(bias_added, b * 4 + (k - 1) + START)
                    sp.dma_start(adj_raw[k % 2][:, :], adj_chunks[b, CHUNKS[k][0], CHUNKS[k][1]]).then_inc(adj_in[k % 2], 16)

            def store_bias(b, groups):
                for i in groups:
                    k, c0 = group_chunk(i)
                    s, g = CHUNKS[k]
                    sp.wait_ge(bias_cut, b * H + i + 1 + START)
                    sp.dma_start(bias_dram[b, c0:c0 + 4, :, g, s, :].rearrange("c p q -> p c q"),
                                 bias_t[i % 2][:, :].rearrange("p (c q) -> p c q", c=4)).then_inc(bias_stored[i % 2], 16)

            def load_bias(h, b, pairs):
                for p in pairs:
                    if isinstance(h, int) and h == 0 and p == 0:
                        for u in range(2):
                            sp.wait_ge(bias_stored[u], (b + 1) * (H // 2) * 16)
                        sp.sem_inc(sp_met, 1)
                    if not (isinstance(h, int) and isinstance(b, int) and h == b == 0 and p < 2):
                        sp.wait_ge(logits_ready, unit(h, b, 2 * p - 2) + START)
                    sp.dma_start(bias[p % 2][:, :, :], bias_dram[b, 2 * p:2 * p + 2].rearrange(
                        "c p k s q -> p c (k s q)")).then_inc(bias_in[p % 2], 16)

            def head(h, first, last):
                if not first:
                    load_bias(h, 0, range(2))
                    for pair in range(2, PAIRS):
                        load_w(h, pair)
                    if not last:
                        load_x(h + 1)
                        load_w(h + 1, 0)
                load_wq(h, 2, 2)
                load_bias(h, 0, range(2, PAIRS))
                if first:
                    load_adj(2, range(2))
                if not last:
                    load_w(h + 1, 1)
                if first:
                    for s in range(ST):
                        sp.dma_start(acc[:, s], x_halves[s].rearrange("r (b e) -> r b e", b=H)).then_inc(acc_in, 16)

                def block_of_queries(b, wq_source, wq_b, making):
                    load_bias(h, b, range(2))
                    if making:
                        load_adj(b + 1, range(2, 3))
                    load_bias(h, b, range(2, 3))
                    if wq_source is not None:
                        load_wq(h, wq_b, wq_source)
                    if making:
                        store_bias(b + 1, range(2))
                    load_bias(h, b, range(3, PAIRS))
                    if making:
                        load_adj(b + 1, range(3, 4))
                        store_bias(b + 1, range(2, H))
                        if not (isinstance(b, int) and b == H - 2):
                            load_adj(b + 2, range(2))

                with sp.Fori(1, H - 2) as b:
                    block_of_queries(b, b + 2, b + 2, first)
                block_of_queries(H - 2, None if last else 0, H, first)
                block_of_queries(H - 1, None if last else 1, H + 1, False)

            sp.dma_start(xrows[:, :, :], x_heads[0]).then_inc(xrows_in, 16)
            load_w(0, 0)
            sp.dma_start(wo_raw[:, :, :], wout_heads[0]).then_inc(wo_in, 16)
            sp.dma_start(wq_raw[:, :, :], wq_blocks[0]).then_inc(wq_in, 16)
            load_adj(0, range(2))
            load_w(0, 1)
            load_w(0, 2)
            load_w(0, LAST)
            load_adj(0, range(2, 3))
            load_wq(0, 1, 1)
            load_adj(0, range(3, 4))
            store_bias(0, range(2))
            load_w(1, 0)
            load_adj(1, range(1))
            store_bias(0, range(2, 4))
            load_adj(1, range(1, 2))
            store_bias(0, range(4, 6))
            load_adj(1, range(2, 3))
            store_bias(0, range(6, 8))
            load_adj(1, range(3, 4))
            load_bias(0, 0, range(2))
            store_bias(1, range(H))
            load_x(1)
            heads(sp, head)
            for blocks in NORM_PARTS:
                for s in reversed(range(ST)):
                    sp.wait_ge(normed[s], blocks.stop)
                    sp.dma_start(out_halves[s].rearrange("r (b e) -> r b e", b=H)[:, blocks],
                                 acc[:, s, blocks, :]).then_inc(stored, 16)
            sp.wait_ge(stored, 16 * ST * len(NORM_PARTS))

        @block.gpsimd
        def _(pool):
            def cut_wq(h, b):
                pool.wait_ge(wq_hi_ready, blk(h, b, 1))
                pool.tensor_tensor(wq_lo[:, :, :], wq_raw[:, :, :], wq_hi[:, :, :],
                                   ALU.subtract).then_inc(wq_lo_ready, 1)

            def add_bias(b, k):
                pool.wait_ge(masked_ready, b * 4 + (k + 1))
                pool.tensor_tensor(masked_chunk(b, k), adj_raw[k % 2][:, :], masked_chunk(b, k), ALU.add).then_inc(bias_added, 1)

            def shift(h, b, c):
                if c == 0:
                    pool.wait_ge(maxes_ready, blk(h, b, 1) + START)
                if isinstance(h, int) and isinstance(b, int) and h == b == 0 and c == 2:
                    pool.wait_ge(w_lo_ready, proj(1, 1, 0, 0))
                if not (isinstance(h, int) and isinstance(b, int) and h == b == 0):
                    pool.wait_ge(pt_lo_ready, unit(h, b, c + 1 - H))
                pool.sem_inc(pool_met, 1)
                pool.tensor_tensor(prob[:, c, :], logits_sb[:, c, :], maxes[:, :, :].rearrange("p t q -> p (t q)"),
                                   ALU.subtract).then_inc(shifted, 1)

            def step(h, b, in_s, in_q, next_wq, first, last):
                for c in range(H):
                    if not (isinstance(h, int) and isinstance(b, int) and h == b == 0):
                        shift(h, b, c)
                    if first and c == H // 2:
                        add_bias(b + 2, 0)
                if first:
                    for k in range(1, 4):
                        add_bias(b + 2, k)
                if in_q == QUERIES and next_wq:
                    cut_wq(h, b + 3)

            for s in STARTED["pool"]:
                pool.sem_inc(s, START)
            pool.memset(ident[:, :], 0.0).then_inc(ident_zero, 1)
            pool.wait_ge(ident_zero, 1)
            pool.affine_select(out=ident[:, :], in_=ident[:, :], compare_op=ALU.not_equal, fill=1.0, base=0,
                               pattern=[[-1, P]], channel_multiplier=1).then_inc(ident_ready, 1)
            pool.memset(half_mask[:, :], 0.5 * MASKED).then_inc(half_mask_ready, 1)
            pool.memset(ones[:, :], 1.0).then_inc(ones_ready, 1)
            cut_wq(0, 0)
            for b in range(2):
                for k in range(4):
                    add_bias(b, k)
            cut_wq(0, 1)
            cut_wq(0, 2)

            def head(h, first, last):
                if not first:
                    cut_wq(h, 1)
                    cut_wq(h, 2)
                if first:
                    for c in range(H):
                        shift(0, 0, c)
                        if c == H // 2:
                            add_bias(2, 0)
                    for k in range(1, 4):
                        add_bias(2, k)
                    cut_wq(0, 3)
                    with pool.Fori(1, H - 3) as b:
                        step(h, b, SCORES, QUERIES, True, first, last)
                    for b in range(H - 3, H):
                        step(h, b, SCORES, QUERIES if b == H - 3 else NOTHING, True, b == H - 3, last)
                else:
                    steps(pool, h, first, last, step)

            heads(pool, head)

        @block.tensor
        def _(pe):
            def product(ps, lhs, rhs, tiles):
                terms = [(a, b, t) for t in range(tiles) for a, b in ((0, 0), (0, 1), (1, 0))]
                for i, (a, b, t) in enumerate(terms):
                    last = pe.matmul(ps, lhs(a, t), rhs(b, t), start=(i == 0), stop=(i == len(terms) - 1))
                return last

            def x_part(b, t):
                return (x_hi, x_lo)[b][:, t, :]

            def transpose_x(h):
                pe.wait_ge(xrows_in, (h + 1) * 16)
                for t in range(KT):
                    for s in range(ST):
                        last = pe.transpose(ps_s[0][:, t * R + s * P:t * R + (s + 1) * P],
                                            xrows[:, s, t * P:(t + 1) * P], ident[:, :])
                last.then_inc(xt_ps, 1)

            def project_kv(h, pair, m, u):
                pe.wait_ge(w_lo_ready, proj(h, pair, m, u) + 1)
                if m and isinstance(pair, int) and pair == LAST:
                    pe.wait_ge(logits_ready, unit(h, 0, H - RING + u) + 1 + START)
                for t in range(KT):
                    last = product(v_bank(pair, m, u)[:, t * R:(t + 1) * R],
                                   lambda a, k: (w_hi, w_lo)[a][m][u][:, k, t * P:(t + 1) * P], x_part, KT)
                last.then_inc(kv_ps, 1)

            def project_vout(h, pair, u):
                if isinstance(pair, int) and pair == u == 0:
                    pe.wait_ge(out_added, blk(h, 0) * ST + START)
                    pe.wait_ge(xw_lo, h * 2 + 2 + START)
                pe.wait_ge(kv_lo, proj(h, pair, 1, u) + 1)
                if u == 0:
                    pe.wait_ge(vp_lo, blk(h, pair * 2) + START)
                if isinstance(pair, int) and pair == LAST - 1 and u == 0:
                    pe.wait_ge(q_lo_ready, blk(h, 0, 1))
                for s in range(ST):
                    last = product(ps_o[u][:, s * d:(s + 1) * d],
                                   lambda a, k: (vt_hi, vt_lo)[a][u][:, k, s * P:(s + 1) * P],
                                   lambda b, k: (wo_hi, wo_lo)[b][:, k, :], KT)
                last.then_inc(vp_ps, 1)

            def project_q(h, b, ps):
                pe.wait_ge(wq_lo_ready, blk(h, b, 1) + START)
                for t in range(KT):
                    last = product(ps[:, t * R:(t + 1) * R],
                                   lambda a, k: (wq_hi, wq_lo)[a][:, k, t * P:(t + 1) * P], x_part, KT)
                last.then_inc(q_ps, 1)

            def scores(c):
                for t in range(ST):
                    last = product(ps_s[c % RING][:, t * R:(t + 1) * R],
                                   lambda a, k: (k_hi, k_lo)[a][:, k, c * R + t * P:c * R + (t + 1) * P],
                                   lambda b, k: (q_hi, q_lo)[b][:, k, :], KT)
                last.then_inc(scores_ps, 1)

            def weigh_values(h, b, c):
                if c == 0:
                    pe.wait_ge(out_added, blk(h, b) * ST + START)
                    pe.wait_ge(vp_lo, blk(h, H) + START)
                pe.wait_ge(pt_hi_ready, unit(h, b, c) + 1)
                tiles = [(s, t) for s in range(ST) for t in range(ST)]
                for s, t in tiles:
                    k, hi = c * ST + t, pt_hi[c % 2][:, t * R + s * P:t * R + (s + 1) * P]
                    pe.matmul(ps_o[s][:, 0:d + ONES], hi, v_hi[:, k, :], start=(k == 0), stop=False)
                    pe.matmul(ps_o[s][:, 0:d], hi, v_lo[:, k, :], start=False, stop=False)
                pe.wait_ge(pt_lo_ready, unit(h, b, c) + 1)
                for s, t in tiles:
                    k, lo = c * ST + t, pt_lo[c % 2][:, t * R + s * P:t * R + (s + 1) * P]
                    last = pe.matmul(ps_o[s][:, 0:d + ONES], lo, v_hi[:, k, :], start=False, stop=(k == JT - 1))
                last.then_inc(pv_done, 1)

            def maxes_of(what, h, b):
                if what == "MT":
                    pe.wait_ge(keymax_ready, unit(h, b, H))
                    for s in range(ST):
                        last = pe.transpose(ps_m[:, s * P:(s + 1) * P], keymax[:, s * P:(s + 1) * P], ident[:, :])
                    last.then_inc(keymax_ps, 1)
                else:
                    pe.wait_ge(maxes_ready, blk(h, b) + START)
                    pe.wait_ge(rowmax_ready, blk(h, b, 1))
                    for s in range(ST):
                        last = pe.transpose(ps_m[:, R + s * P:R + (s + 1) * P],
                                            rowmax[:, s:s + 1].to_broadcast([P, P]), ident[:, :])
                    last.then_inc(maxes_ps, 1)

            def transpose_bias(b, i):
                k, c0 = group_chunk(i)
                pe.wait_ge(bias_cut, b * H + i + START)
                pe.wait_ge(bias_added, b * 4 + (k + 1) + START)
                for j in range(4):
                    last = pe.transpose(ps_b[:, j * P:(j + 1) * P],
                                        masked_chunk(b, k).rearrange("p (k c) -> p c k", c=H)[:, c0 + j, :], ident[:, :])
                last.then_inc(bias_ps, 1)

            def step(h, b, in_s, in_q, next_wq, first, last):
                for what, c in ORDER:
                    if what == "PV":
                        weigh_values(h, b, c)
                    elif what in ("MT", "MB") and in_s == SCORES:
                        maxes_of(what, h, b + 1)
                    elif what == "S" and in_s == SCORES:
                        if c == 0:
                            pe.wait_ge(q_lo_ready, blk(h, b, 2))
                        pe.wait_ge(logits_ready, unit(h, b + 1, c - RING) + 1 + START)
                        scores(c)
                    elif what == "S" and in_s == NEXT_KV:
                        for m, u in KV[c:c + 1]:
                            if m == u == 0:
                                pe.wait_ge(xw_lo, h * 2 + 3 + START)
                                pe.wait_ge(logits_ready, unit(h, H, 0) + START)
                            project_kv(h + 1, 0, m, u)
                    elif what == "Q" and in_q != NOTHING:
                        pe.wait_ge(logits_ready, unit(h, b + 1, H - RING) + 1 + START)
                        if in_q == QUERIES:
                            project_q(h, b + 2, ps_s[0])
                        else:
                            transpose_x(h + 1)
                    if first and (what, c) in BIAS_AT:
                        transpose_bias(b + 2, BIAS_AT.index((what, c)))

            def head(h, first, last):
                def queries(h, b):
                    if b == 0:
                        pe.wait_ge(out_added, blk(h, 0) * ST + START)
                        pe.wait_ge(vp_lo, blk(h, 2 * LAST - 2) + START)
                        project_q(h, 0, ps_o[0])
                    else:
                        pe.wait_ge(logits_ready, unit(h, 0, H - 2) + 1 + START)
                        project_q(h, 1, ps_s[2])

                def first_scores(h, b, c):
                    if c < 2:
                        pe.wait_ge(kv_lo, proj(h, LAST, 0, c) + 1)
                    if c >= RING:
                        pe.wait_ge(logits_ready, unit(h, 0, c - RING) + 1 + START)
                    scores(c)

                phase_a(pe, h, first, project_vout, project_kv, queries, first_scores, maxes_of,
                        spares(bias_groups(transpose_bias)) if first else lambda: None)
                steps(pe, h, first, last, step)

            for s in STARTED["pe"]:
                pe.sem_inc(s, START)
            pe.wait_ge(ident_ready, 1)
            transpose_x(0)
            pe.wait_ge(xw_lo, 1 + START)
            for m, u in KV:
                project_kv(0, 0, m, u)
            heads(pe, head)

        @block.scalar
        def _(act):
            def cut_weight(h, pair, m, u):
                act.wait_ge(*weights_loaded(h, pair, m))
                act.activation(w_hi[m][u][:, :, :], weights_buffer(h, pair, m, u), ACT.Copy).then_inc(w_hi_ready, 1)

            def cut_wq(h, b):
                act.wait_ge(wq_in, blk(h, b, 1) * 16)
                act.wait_ge(q_ps, blk(h, b) + START)
                act.activation(wq_hi[:, :, :], wq_raw[:, :, :], ACT.Copy).then_inc(wq_hi_ready, 1)

            def cut_x(h):
                act.wait_ge(xt_ps, h + 1 + START)
                act.activation(x_hi[:, :, :], halves(ps_s[0]), ACT.Copy).then_inc(xw_hi, 1)

            def cut_wout(h):
                act.wait_ge(wo_in, (h + 1) * 16)
                act.activation(wo_hi[:, :, :], wo_raw[:, :, :], ACT.Copy).then_inc(xw_hi, 1)

            def cut_kv(h, pair, m, u, next_pair, last=False):
                act.wait_ge(kv_ps, proj(h, pair, m, u) + 1)
                dst = vt_hi[u][:, :, :] if m else k_hi[:, :, bass.ds((pair * 2 + u) * R, R)]
                act.activation(dst, halves(v_bank(pair, m, u)), ACT.Copy).then_inc(kv_hi, 1)
                if not last:
                    cut_weight(h, next_pair, m, u)

            def cut_vout(h, pair, u):
                act.wait_ge(vp_ps, blk(h, pair * 2, u + 1))
                act.activation(v_hi[:, bass.ds((pair * 2 + u) * ST, ST), 0:d], halves(ps_o[u]), ACT.Copy).then_inc(vp_hi, 1)

            def cut_q(h, b, ps):
                act.wait_ge(q_ps, blk(h, b, 1) + START)
                act.activation(q_hi[:, :, :], halves(ps), ACT.Copy, scale=QSCALE).then_inc(q_hi_ready, 1)

            def exps(h, b, c):
                act.wait_ge(shifted, unit(h, b, c) + 1)
                act.activation(prob[:, c, :], prob[:, c, :], ACT.Exp, scale=2.0).then_inc(exp_ready, 1)

            def cut_exps(h, b, c):
                act.wait_ge(exp_ready, unit(h, b, c) + 1)
                act.wait_ge(pv_done, unit(h, b, c) - 1 + START)
                act.activation(pt_hi[c % 2][:, :], prob[:, c, :], ACT.Copy).then_inc(pt_hi_ready, 1)

            def copy_maxes(what, h, b):
                if what == "MB":
                    if not (isinstance(h, int) and isinstance(b, int) and h == b == 0):
                        act.wait_ge(shifted, unit(h, b, 0))
                    act.wait_ge(maxes_ps, blk(h, b, 1))
                    act.activation(maxes[:, :, :], ps_m[:, R:2 * R].unsqueeze(1).to_broadcast([P, 2, R]),
                                   ACT.Copy).then_inc(maxes_ready, 1)

            def copy_bias(b, i):
                if not (isinstance(b, int) and b == 0 and i < 2):
                    act.wait_ge(bias_stored[i % 2], (b * (H // 2) + i // 2) * 16)
                act.wait_ge(bias_ps, b * H + i + 1)
                act.activation(bias_t[i % 2][:, :], ps_b[:, :], ACT.Copy).then_inc(bias_cut, 1)

            def step(h, b, in_s, in_q, next_wq, first, last):
                exps(h, b, 0)
                cut_exps(h, b, 0)
                if first:
                    exps(h, b, 1)
                    cut_exps(h, b, 1)
                for what, c in ORDER:
                    if (what, c) in CUT_AT and not (first and CUT_AT[what, c] == 1):
                        cut_exps(h, b, CUT_AT[what, c])
                    if what == "MB" and in_s == SCORES:
                        copy_maxes(what, h, b + 1)
                    if what == "S" and c + 1 < H and not (first and c == 0):
                        exps(h, b, c + 1)
                    if what == "S" and in_s == NEXT_KV:
                        for m, u in KV[c:c + 1]:
                            cut_kv(h + 1, 0, m, u, 1)
                    elif what == "Q" and in_q == QUERIES:
                        cut_q(h, b + 2, ps_s[0])
                    elif (what, c) == ("PV", H - 3) and in_q == QUERIES and next_wq:
                        cut_wq(h, b + 3)
                    elif what == "Q" and in_q == NEXT_X:
                        cut_x(h + 1)
                        cut_wout(h + 1)
                    if first and (what, c) in BIAS_AT:
                        copy_bias(b + 2, BIAS_AT.index((what, c)))

            def head(h, first, last):
                def kv(h, pair, m, u):
                    if isinstance(pair, int) and pair == LAST:
                        cut_kv(h, LAST, m, u, 0, True)
                        if not last:
                            cut_weight(h + 1, 0, m, u)
                    else:
                        cut_kv(h, pair, m, u, pair + 1)

                def queries(h, b):
                    cut_q(h, b, ps_s[2] if b else ps_o[0])
                    cut_wq(h, b + 1)

                phase_a(act, h, first, cut_vout, kv, queries, lambda h, b, c: None, copy_maxes,
                        spares(bias_groups(copy_bias)) if first else lambda: None)
                steps(act, h, first, last, step)

            for s in STARTED["act"]:
                act.sem_inc(s, START)
            cut_x(0)
            for m, u in KV:
                cut_weight(0, 0, m, u)
            cut_wout(0)
            cut_wq(0, 0)
            act.wait_ge(ones_ready, 1)
            act.activation(v_hi[:, :, d:d + ONES], ones[:, 0:1].to_broadcast([P, JT * ONES]).rearrange("p (j o) -> p j o", j=JT),
                           ACT.Copy)
            for m, u in KV:
                cut_kv(0, 0, m, u, 1)
            heads(act, head)
            for part, blocks in enumerate(NORM_PARTS):
                act.wait_ge(veps_ready, part + 1)
                act.activation(std[:, :, blocks], veps[:, :, blocks], ACT.Sqrt).then_inc(std_ready, 1)
                act.wait_ge(norm_bias_ready, part + 1)
                for b in range(blocks.start, blocks.stop):
                    act.activation(acc[:, 1, b, :], acc[:, 1, b, :], ACT.Identity, bias=norm_bias[:, 1, b:b + 1],
                                   scale=rstd[:, 1, b:b + 1]).then_inc(normed[1], 1)

        @block.vector
        def _(dve):
            def cut_weight(h, pair, m, u):
                dve.wait_ge(w_hi_ready, proj(h, pair, m, u) + 1)
                dve.tensor_tensor(w_lo[m][u][:, :, :], weights_buffer(h, pair, m, u), w_hi[m][u][:, :, :],
                                  ALU.subtract).then_inc(w_lo_ready, 1)

            def cut_x(h):
                dve.wait_ge(xw_hi, h * 2 + 1)
                dve.tensor_tensor(x_lo[:, :, :], halves(ps_s[0]), x_hi[:, :, :], ALU.subtract).then_inc(xw_lo, 1)

            def cut_wout(h):
                dve.wait_ge(xw_hi, h * 2 + 2)
                dve.tensor_tensor(wo_lo[:, :, :], wo_raw[:, :, :], wo_hi[:, :, :], ALU.subtract).then_inc(xw_lo, 1)

            def cut_kv(h, pair, m, u, next_pair, last=False):
                dve.wait_ge(kv_hi, proj(h, pair, m, u) + 1)
                cols = bass.ds((pair * 2 + u) * R, R)
                hi, dst = ((vt_hi[u][:, :, :], vt_lo[u][:, :, :]) if m else (k_hi[:, :, cols], k_lo[:, :, cols]))
                dve.tensor_tensor(dst, halves(v_bank(pair, m, u)), hi, ALU.subtract).then_inc(kv_lo, 1)
                if not last:
                    cut_weight(h, next_pair, m, u)

            def cut_vout(h, pair, u):
                dve.wait_ge(vp_hi, blk(h, pair * 2, u + 1))
                tiles = bass.ds((pair * 2 + u) * ST, ST)
                dve.tensor_tensor(v_lo[:, tiles, :], halves(ps_o[u]), v_hi[:, tiles, 0:d], ALU.subtract).then_inc(vp_lo, 1)

            def cut_q(h, b, ps):
                dve.wait_ge(q_hi_ready, blk(h, b, 1))
                dve.scalar_tensor_tensor(q_lo[:, :, :], halves(ps), QSCALE, q_hi[:, :, :],
                                         ALU.mult, ALU.subtract).then_inc(q_lo_ready, 1)

            def cut_exps(h, b, c):
                dve.wait_ge(pt_hi_ready, unit(h, b, c) + 1)
                dve.tensor_tensor(pt_lo[c % 2][:, :], prob[:, c, :], pt_hi[c % 2][:, :], ALU.subtract).then_inc(pt_lo_ready, 1)

            def mask(b, k):
                s, g = CHUNKS[k]
                dve.wait_ge(adj_in[k % 2], (b * 2 + k // 2 + 1) * 16)
                if not (isinstance(b, int) and (b == 0 or b == 1 and k < 2)):
                    dve.wait_ge(bias_ps, b * H + (k - 1) * QUADS)
                if g == 0:
                    dve.wait_ge(keep_steps, b * 4 + 2 * s + START)
                dve.scalar_tensor_tensor(masked_chunk(b, k), adj_raw[k % 2][:, :], 0.0,
                                         half_mask[:, 0:1].to_broadcast([P, CHUNK]), ALU.is_equal, ALU.mult,
                                         accum_out=mask_sum[:, g:g + 1]).then_inc(masked_ready, 1)
                if g == ST - 1:
                    dve.wait_ge(masked_ready, b * 4 + (k + 1))
                    dve.tensor_reduce(mask_max[:, :], mask_sum[:, :], AX.X, ALU.max).then_inc(keep_steps, 1)
                    dve.wait_ge(keep_steps, b * 4 + (2 * s + 1) + START)
                    dve.tensor_scalar(keep[:, s, bass.ds(b, 1)], mask_max[:, :], 0.5 * MASKED * CHUNK, None,
                                      ALU.is_gt).then_inc(keep_steps, 1)

            def logits(h, b, c):
                if c % 2 == 0:
                    p = c // 2
                    dve.wait_ge(bias_in[p % 2], (blk(h, b) * (H // 4) + (p // 2 + 1)) * 16)
                if not (isinstance(h, int) and isinstance(b, int) and h == b == 0):
                    dve.wait_ge(shifted, unit(h, b, c + 1 - H))
                dve.wait_ge(scores_ps, unit(h, b, c) + 1)
                dve.tensor_tensor(logits_sb[:, c, :], ps_s[c % RING][:, :], bias[c // 2 % 2][:, c % 2, :],
                                  ALU.add).then_inc(logits_ready, 1)
                if c == 1:
                    if not (isinstance(h, int) and isinstance(b, int) and h == b == 0):
                        dve.wait_ge(keymax_ps, blk(h, b))
                elif c > 1:
                    dve.wait_ge(keymax_ready, unit(h, b, c - 1))
                if c:
                    dve.wait_ge(logits_ready, unit(h, b, c + 1) + START)
                    dve.tensor_tensor(keymax[:, :], logits_sb[:, c, :], logits_sb[:, 0, :] if c == 1 else keymax[:, :],
                                      ALU.max).then_inc(keymax_ready, 1)
                if c == H - 1:
                    dve.wait_ge(keymax_ready, unit(h, b, c))
                    dve.tensor_tensor(keymax[:, 0:R], keymax[:, 0:R], keymax[:, R:2 * R], ALU.max).then_inc(keymax_ready, 1)

            def reduce_maxes(what, h, b):
                if what == "MT":
                    dve.wait_ge(keymax_ps, blk(h, b, 1))
                    dve.tensor_reduce(rowmax[:, :], ps_m[:, 0:R].rearrange("p (s k) -> p s k", s=ST), AX.X,
                                      ALU.max).then_inc(rowmax_ready, 1)

            def add_tiles(h, b):
                dve.wait_ge(pv_done, unit(h, b, H) + START)
                for s in range(ST):
                    dve.reciprocal(rdenom[:, s:s + 1], ps_o[s][:, d:d + 1]).then_inc(rdenom_ready, 1)
                for s in range(ST):
                    dve.wait_ge(rdenom_ready, blk(h, b) * ST + s + 1)
                    dve.tensor_tensor(weight[:, s:s + 1], rdenom[:, s:s + 1], keep[:, s, bass.ds(b, 1)],
                                      ALU.mult).then_inc(weight_ready, 1)
                for s in range(ST):
                    dve.wait_ge(weight_ready, blk(h, b) * ST + s + 1)
                    a = acc[:, s, b, :]
                    dve.scalar_tensor_tensor(a, ps_o[s][:, 0:d], weight[:, s:s + 1], a,
                                             ALU.mult, ALU.add).then_inc(out_added, 1)

            def row_stats(b):
                for s in range(ST):
                    dve.wait_ge(out_added, blk(H - 1, b) * ST + (s + 1) + START)
                    dve.bn_stats(stats[:, s, b, :], acc[:, s, b, :]).then_inc(stats_ready, 1)

            def variances(blocks):
                dve.wait_ge(stats_ready, blocks.stop * ST)
                for b in range(blocks.start, blocks.stop):
                    for s in range(ST):
                        dve.bn_aggr(moments[:, s, b, :], stats[:, s, b, :]).then_inc(moments_ready, 1)
                dve.wait_ge(moments_ready, blocks.stop * ST)
                dve.tensor_scalar(veps[:, :, blocks], moments[:, :, blocks, 1], EPS, None, ALU.add).then_inc(veps_ready, 1)

            def norm_factors(part, blocks):
                dve.wait_ge(std_ready, part + 1)
                dve.reciprocal(rstd[:, :, blocks], std[:, :, blocks]).then_inc(rstd_ready, 1)
                dve.wait_ge(rstd_ready, part + 1)
                dve.scalar_tensor_tensor(norm_bias[:, :, blocks], moments[:, :, blocks, 0], -1.0, rstd[:, :, blocks],
                                         ALU.mult, ALU.mult).then_inc(norm_bias_ready, 1)

            def normalise(blocks):
                for b in range(blocks.start, blocks.stop):
                    dve.tensor_scalar(acc[:, 0, b, :], acc[:, 0, b, :], moments[:, 0, b, 0:1],
                                      rstd[:, 0, b:b + 1], ALU.subtract, ALU.mult).then_inc(normed[0], 1)

            def step(h, b, in_s, in_q, next_wq, first, last):
                cut_exps(h, b, 0)
                if first:
                    cut_exps(h, b, 1)
                    mask(b + 2, 0)
                    mask(b + 2, 1)
                for what, c in ORDER:
                    if what == "MT" and in_s == SCORES:
                        reduce_maxes(what, h, b + 1)
                    if (what, c) in CUT_AT and not (first and CUT_AT[what, c] == 1):
                        cut_exps(h, b, CUT_AT[what, c])
                    if first and (what, c) in MASK_AT:
                        mask(b + 2, MASK_AT[what, c])
                    if what == "S" and in_s == SCORES:
                        logits(h, b + 1, c)
                    elif what == "S" and in_s == NEXT_KV:
                        for m, u in KV[c:c + 1]:
                            cut_kv(h + 1, 0, m, u, 1)
                    elif what == "Q" and in_q == QUERIES:
                        cut_q(h, b + 2, ps_s[0])
                    elif what == "Q" and in_q == NEXT_X:
                        cut_x(h + 1)
                        cut_wout(h + 1)
                if isinstance(h, int) and h == 0:
                    dve.wait_ge(acc_in, 16 * ST)
                ending = last and isinstance(b, int) and b == H - 1
                if ending:
                    norm_factors(0, NORM_PARTS[0])
                add_tiles(h, b)
                if last:
                    row_stats(b)
                if last and isinstance(b, int) and b >= H - 2:
                    variances(NORM_PARTS[b - (H - 2)])
                if ending:
                    normalise(NORM_PARTS[0])

            def head(h, first, last):
                def kv(h, pair, m, u):
                    if isinstance(pair, int) and pair == LAST:
                        cut_kv(h, LAST, m, u, 0, True)
                        if not last:
                            cut_weight(h + 1, 0, m, u)
                    else:
                        cut_kv(h, pair, m, u, pair + 1)

                def masks(e):
                    if e % 2 == 0 and 4 <= e + 2 < 16:
                        mask((e + 2) // 2 // 4, (e + 2) // 2 % 4)

                phase_a(dve, h, first, cut_vout, kv, lambda h, b: cut_q(h, b, ps_s[2] if b else ps_o[0]), logits,
                        reduce_maxes, spares(masks) if first else lambda: None, maxes_early=True)
                steps(dve, h, first, last, step)

            for s in STARTED["dve"]:
                dve.sem_inc(s, START)
            dve.wait_ge(half_mask_ready, 1)
            cut_x(0)
            for m, u in KV:
                cut_weight(0, 0, m, u)
            cut_wout(0)
            for m, u in KV:
                cut_kv(0, 0, m, u, 1)
                if u == 0:
                    mask(0, m)
            heads(dve, head)

            norm_factors(1, NORM_PARTS[1])
            normalise(NORM_PARTS[1])


_INPUTS = ["x", "adj", "L0_gnn_Wq", "L0_gnn_Wk", "L0_gnn_Wv", "L0_gnn_Wout"]


def kernel(**inputs):
    import numpy as np
    import concourse.bacc as bacc
    from concourse.bass_utils import run_bass_kernel_spmd

    nc = bacc.Bacc("TRN2", target_bir_lowering=False, num_devices=1)
    arrays, args = {}, []
    for name in _INPUTS:
        a = np.ascontiguousarray(inputs[name])
        arrays[f"in_{name}"] = a
        args.append(nc.dram_tensor(f"in_{name}", a.shape, mybir.dt.from_np(a.dtype), kind="ExternalInput").ap())
    out = nc.dram_tensor("out", arrays["in_x"].shape, F32, kind="ExternalOutput").ap()
    attention_layer_norm(nc, *args, out)
    r = run_bass_kernel_spmd(nc, [arrays], core_ids=[0])
    return r.results[0]["out"]
```
